# Optimizing a Trainium2 kernel written in Bass

```python
import numpy as np
import jax
import jax.numpy as jnp

def _softmax(x, axis=-1):
    return jax.nn.softmax(x, axis=axis)

def _gelu(x):
    return jax.nn.gelu(x, approximate=True)

def _silu(x):
    return jax.nn.silu(x)

def _sigmoid(x):
    return jax.nn.sigmoid(x)

def _layernorm(x, axis=-1, eps=1e-05):
    m = jnp.mean(x, axis=axis, keepdims=True)
    v = jnp.var(x, axis=axis, keepdims=True)
    return (x - m) / jnp.sqrt(v + eps)

def _scatter_add(tgt, idx, src, axis=0):
    return tgt.at[idx].add(src)

def _segment_sum(src, seg, n):
    return jax.ops.segment_sum(src, seg, n)
kernel_name = 'mk_sandwich_d1_jaxref_r8_c21502'

def setup_inputs(seed: int=0):
    np.random.seed(seed)
    _w = jnp.asarray

    def _L0_attn_setup():
        import jax, jax.numpy as jnp
        import numpy as np
        Q_DIM = 512
        N_HEADS = 32
        HEAD_DIM = 128
        INNER = N_HEADS * HEAD_DIM
        EPS = 1e-06

        def rms_norm(x, w):
            xf = x.astype(jnp.float32)
            var = jnp.mean(xf * xf, axis=-1, keepdims=True)
            return (w.astype(jnp.float32) * xf * jax.lax.rsqrt(var + EPS)).astype(x.dtype)
        key = jax.random.key(seed)
        ks = jax.random.split(key, 12)
        s = 1.0 / np.sqrt(Q_DIM)
        return {'hidden_states': jax.random.normal(ks[0], (2, 256, Q_DIM), dtype=jnp.float32), 'Wq': jax.random.normal(ks[1], (Q_DIM, INNER), dtype=jnp.float32) * s, 'bq': jnp.zeros((INNER,), dtype=jnp.float32), 'Wk': jax.random.normal(ks[2], (Q_DIM, INNER), dtype=jnp.float32) * s, 'bk': jnp.zeros((INNER,), dtype=jnp.float32), 'Wv': jax.random.normal(ks[3], (Q_DIM, INNER), dtype=jnp.float32) * s, 'bv': jnp.zeros((INNER,), dtype=jnp.float32), 'Wo': jax.random.normal(ks[4], (INNER, Q_DIM), dtype=jnp.float32) * s, 'bo': jnp.zeros((Q_DIM,), dtype=jnp.float32), 'gq': jnp.ones((INNER,), dtype=jnp.float32), 'gk': jnp.ones((INNER,), dtype=jnp.float32)}
    _L0_attn_in = _L0_attn_setup()

    def _L0_ffn_setup():
        import jax, jax.numpy as jnp
        import numpy as np
        MAX_THRESHOLD = 1.0 / 8.0
        SCALING = 32.0 / 16.0
        key = jax.random.key(seed)
        ks = jax.random.split(key, 8)
        B_, S, D, O, E, R = (4, 256, 512, 512, 8, 16)
        sd = 1.0 / np.sqrt(D)
        return {'x': jax.random.normal(ks[0], (B_, S, D), jnp.float32), 'W_base': jax.random.normal(ks[1], (O, D), jnp.float32) * sd, 'b_base': jax.random.normal(ks[2], (O,), jnp.float32) * 0.01, 'W_gate': jax.random.normal(ks[3], (E, D), jnp.float32) * sd, 'W_thr': jax.random.normal(ks[4], (1, D), jnp.float32) * sd, 'b_thr': jax.random.normal(ks[5], (1,), jnp.float32) * 0.01, 'A': jax.random.normal(ks[6], (E, R, D), jnp.float32) * sd, 'B': jax.random.normal(ks[7], (O,), jnp.float32)[None, :, None] * jnp.zeros((E, O, R), jnp.float32) + jax.random.normal(jax.random.fold_in(key, 7), (E, O, R), jnp.float32) * (1.0 / np.sqrt(R))}
    _L0_ffn_in = _L0_ffn_setup()
    _d = {'L0_attn_hidden_states': _L0_attn_in['hidden_states'], 'L0_attn_Wq': _L0_attn_in['Wq'], 'L0_attn_bq': _L0_attn_in['bq'], 'L0_attn_Wk': _L0_attn_in['Wk'], 'L0_attn_bk': _L0_attn_in['bk'], 'L0_attn_Wv': _L0_attn_in['Wv'], 'L0_attn_bv': _L0_attn_in['bv'], 'L0_attn_Wo': _L0_attn_in['Wo'], 'L0_attn_bo': _L0_attn_in['bo'], 'L0_attn_gq': _L0_attn_in['gq'], 'L0_attn_gk': _L0_attn_in['gk'], 'L0_ffn_W_base': _L0_ffn_in['W_base'], 'L0_ffn_b_base': _L0_ffn_in['b_base'], 'L0_ffn_W_gate': _L0_ffn_in['W_gate'], 'L0_ffn_W_thr': _L0_ffn_in['W_thr'], 'L0_ffn_b_thr': _L0_ffn_in['b_thr'], 'L0_ffn_A': _L0_ffn_in['A'], 'L0_ffn_B': _L0_ffn_in['B']}
    _x0 = _d['L0_attn_hidden_states']
    _d['L0_attn_hidden_states'] = jax.random.normal(jax.random.fold_in(jax.random.key(seed), 1), (2, 512, 512), dtype=_x0.dtype)
    del _x0
    return _d

def reference(L0_attn_hidden_states, L0_attn_Wq, L0_attn_bq, L0_attn_Wk, L0_attn_bk, L0_attn_Wv, L0_attn_bv, L0_attn_Wo, L0_attn_bo, L0_attn_gq, L0_attn_gk, L0_ffn_W_base, L0_ffn_b_base, L0_ffn_W_gate, L0_ffn_W_thr, L0_ffn_b_thr, L0_ffn_A, L0_ffn_B):

    def _L0_attn_ref(hidden_states, Wq, bq, Wk, bk, Wv, bv, Wo, bo, gq, gk):
        import jax, jax.numpy as jnp
        import numpy as np
        Q_DIM = 512
        N_HEADS = 32
        HEAD_DIM = 128
        INNER = N_HEADS * HEAD_DIM
        EPS = 1e-06

        def rms_norm(x, w):
            xf = x.astype(jnp.float32)
            var = jnp.mean(xf * xf, axis=-1, keepdims=True)
            return (w.astype(jnp.float32) * xf * jax.lax.rsqrt(var + EPS)).astype(x.dtype)
        B, S, _ = hidden_states.shape
        q = hidden_states @ Wq + bq
        k = hidden_states @ Wk + bk
        v = hidden_states @ Wv + bv
        q = rms_norm(q, gq)
        k = rms_norm(k, gk)
        q = q.reshape(B, S, N_HEADS, HEAD_DIM).transpose(0, 2, 1, 3)
        k = k.reshape(B, S, N_HEADS, HEAD_DIM).transpose(0, 2, 1, 3)
        v = v.reshape(B, S, N_HEADS, HEAD_DIM).transpose(0, 2, 1, 3)
        scale = 1.0 / np.sqrt(HEAD_DIM)
        attn = jnp.einsum('bhqd,bhkd->bhqk', q.astype(jnp.float32), k.astype(jnp.float32)) * scale
        attn = jax.nn.softmax(attn, axis=-1)
        out = jnp.einsum('bhqk,bhkd->bhqd', attn, v.astype(jnp.float32))
        out = out.transpose(0, 2, 1, 3).reshape(B, S, INNER).astype(hidden_states.dtype)
        return out @ Wo + bo

    def _L0_ffn_ref(x, W_base, b_base, W_gate, W_thr, b_thr, A, B):
        import jax, jax.numpy as jnp
        import numpy as np
        MAX_THRESHOLD = 1.0 / 8.0
        SCALING = 32.0 / 16.0
        base = jnp.einsum('bsd,od->bso', x, W_base) + b_base
        D = x.shape[-1]
        xf = x.reshape(-1, D)
        gate_logits = jax.nn.softmax(xf @ W_gate.T, axis=-1)
        thresholds = jax.nn.sigmoid(xf @ W_thr.T + b_thr) * MAX_THRESHOLD
        adapted = gate_logits - thresholds
        selected = (adapted >= 0).astype(x.dtype)
        weights = adapted * selected
        wsum = jnp.sum(weights, axis=-1, keepdims=True)
        wsum = jnp.where(wsum == 0, jnp.ones_like(wsum), wsum)
        weights = weights / wsum
        h = jnp.einsum('nd,erd->ner', xf, A)
        moe = jnp.einsum('ner,ne,eor->no', h, weights, B) * SCALING
        out = base + moe.reshape(base.shape)
        return out
    x = L0_attn_hidden_states
    x = x + _layernorm(_L0_attn_ref(_layernorm(x, axis=-1), L0_attn_Wq, L0_attn_bq, L0_attn_Wk, L0_attn_bk, L0_attn_Wv, L0_attn_bv, L0_attn_Wo, L0_attn_bo, L0_attn_gq, L0_attn_gk), axis=-1)
    x = x + _layernorm(_L0_ffn_ref(_layernorm(x, axis=-1), L0_ffn_W_base, L0_ffn_b_base, L0_ffn_W_gate, L0_ffn_W_thr, L0_ffn_b_thr, L0_ffn_A, L0_ffn_B), axis=-1)
    return x

_drawn_inputs = setup_inputs


def setup_inputs(seed=0):
    import zlib

    import numpy as np

    out = dict(_drawn_inputs(seed))
    spreads = {'L0_attn_bq': (0.0, 0.1),
     'L0_attn_bk': (0.0, 0.8),
     'L0_attn_bv': (0.0, 0.1),
     'L0_attn_bo': (0.0, 0.1),
     'L0_attn_gq': (1.0, 0.2),
     'L0_attn_gk': (1.0, 0.2)}
    factors = {'L0_ffn_b_base': 8.0}
    for name, (base, spread) in spreads.items():
        noise = np.random.default_rng([zlib.crc32(name.encode()), seed]).standard_normal(out[name].shape)
        drawn = base * np.exp(spread * noise) if base else spread * noise
        out[name] = jnp.asarray(drawn.astype(out[name].dtype))
    for name, factor in factors.items():
        out[name] = (out[name] * factor).astype(out[name].dtype)
    return out
```

```python
from contextlib import ExitStack

import concourse.bass as bass
from concourse import mybir

F32 = mybir.dt.float32
F32R = mybir.dt.float32r
ALU = mybir.AluOpType
ACT = mybir.ActivationFunctionType
AX = mybir.AxisListType

P = 128


def build(nc, x, w_qk, w_v, w_o, tables, bo, w_base, w_in, b_t, b_base, b_thr, out):
    NT = x.shape[0]
    D = x.shape[2]
    C = D // P
    HEADS = w_qk.shape[0]
    INNER = HEADS * P
    PAIRS = HEADS // 2
    TB = NT // 2
    S = TB * P
    TOK = NT * P
    E = 8
    R = P // E
    IN = P + E + 1
    WIDE = 2 * P
    LN_EPS, RMS_EPS = 1e-5, 1e-6
    SCORE_SCALE = float(P) ** -0.5
    assert C == TB == 4 and S == 512

    FIRST = [(par, g) for b in range(2) for par in range(2) for g in (2 * b, 2 * b + 1)]

    q_k_scratch = nc.dram_tensor("q_k_scratch", [HEADS, P, 2, TOK], F32, kind="Internal").ap()

    with ExitStack() as ctx:
        def sb(name, shape, dt=F32, stack=ctx):
            return stack.enter_context(nc.sbuf_tensor(name, shape, dt))

        def sem(name):
            return ctx.enter_context(nc.semaphore(name))

        ps = ctx.enter_context(nc.psum_tensor("ps", [P, 8, 512], F32))
        SCORE, TRANS, WORK = 0, 4, 6

        HIDDEN = 4
        HW = 6

        y = sb("y", [P, NT, D])
        xh = sb("xh", [P, C, TOK], F32R)
        xl = sb("xl", [P, C, TOK], F32R)
        ident = sb("ident", [P, P])
        ones = sb("ones", [P, P])
        tab = sb("tab", [P, 5, HEADS])
        wv_stage = sb("wv_stage", [P, C, 2 * P])
        wv_hi = sb("wv_hi", [P, 2, C, 2 * P], F32R)
        wv_lo = sb("wv_lo", [P, 2, C, 2 * P], F32R)
        wo_stage = sb("wo_stage", [P, 2, D])
        wb_stage = sb("wb_stage", [P, C, D])
        in_stage = sb("in_stage", [P, w_in.shape[1]])
        in_hi = sb("in_hi", [P, w_in.shape[1]], F32R)
        in_lo = sb("in_lo", [P, w_in.shape[1]], F32R)
        bt_stage = sb("bt_stage", [P, D])
        thr_bias = sb("thr_bias", [P, 1])
        stats = sb("stats", [P, 4, NT, 6])
        mv = sb("mv", [P, 4, NT, 2])
        var_eps = sb("var_eps", [P, 4, NT])
        rstd = sb("rstd", [P, 4, NT])
        nmr = sb("nmr", [P, 4, NT])
        sq_eps = sb("sq_eps", [P, 2 * NT])
        q_k_bias = sb("q_k_bias", [P, 2, 2])
        v_bias = sb("v_bias", [P, 2, 1])
        minus_half = sb("minus_half", [P, 2 * NT])
        rms = sb("rms", [P, 2 * NT])
        neg_max = sb("neg_max", [P, 2, TB])
        row_sum = sb("row_sum", [P, 2, TB])
        row_inv = sb("row_inv", [P, 2, TB])

        with ExitStack() as a_only:
            wa_stage = sb("wa_stage", [P, 2, 2, C, P], F32, a_only)
            wa_hi = sb("wa_hi", [P, 2, 2, C, P], F32R, a_only)
            wa_lo = sb("wa_lo", [P, 2, 2, C, P], F32R, a_only)
            qk_out = sb("qk_out", [P, 2, 2, TOK], F32, a_only)
            squares = sb("squares", [P, 2, 2, TOK], F32, a_only)
            acc = sb("acc", [P, 2, TOK], F32, a_only)

        vh = sb("vh", [P, NT, 2 * P], F32R)
        vl = sb("vl", [P, NT, 2 * P], F32R)
        oth = sb("oth", [P, 2, TOK], F32R)
        otl = sb("otl", [P, 2, TOK], F32R)
        pth = sb("pth", [P, TB, S], F32R)
        ptl = sb("ptl", [P, TB, S], F32R)
        wo_hi = sb("wo_hi", [P, 2, 2, D], F32R)
        wo_lo = sb("wo_lo", [P, 2, 2, D], F32R)
        qk_in = sb("qk_in", [P, 4, 2, S])
        qk_hi = sb("qk_hi", [P, 2, 2, S], F32R)
        qk_lo = sb("qk_lo", [P, 2, 2, S], F32R)
        rms_row = sb("rms_row", [P, 2, TOK])
        prob = sb("prob", [P, TB, S])

        diag = prob

        wb_hi = wv_hi[:, :, :, :].rearrange("p a c n -> p (a c n)").rearrange("p (c n) -> p c n", c=C)
        wb_lo = wv_lo[:, :, :, :].rearrange("p a c n -> p (a c n)").rearrange("p (c n) -> p c n", c=C)
        bt_hi, bt_lo = wo_hi[:, 0, 0, :], wo_lo[:, 0, 0, :]
        x_again = qk_in[:, :, :, :].rearrange("p a w n -> p (a w) n")
        z = prob
        hw = rms_row[:, 0, :].rearrange("p (b n) -> p b n", b=2)
        hw_hi, hw_lo = pth, ptl
        bb = wv_stage[:, 0:2, :].rearrange("p a n -> p (a n)")
        g_e = sb("g_e", [P, NT, E])
        g_p = sb("g_p", [P, NT, E])
        g_w = sb("g_w", [P, NT, E])
        g_s = sb("g_s", [P, 10, NT])

        x_loaded = [sem(f"x_loaded{t}") for t in range(NT)]
        tab_loaded = sem("tab_loaded")
        const_ready = sem("const_ready")
        ln_chain = sem("ln_chain")
        nmr_ready = sem("nmr_ready")
        var_ready = sem("var_ready")
        rstd_ready = sem("rstd_ready")
        x_normed = [sem("x_normed0"), sem("x_normed1")]
        x_turned = sem("x_turned")
        xh_ready = sem("xh_ready")
        xl_ready = sem("xl_ready")
        wa_loaded = [sem("wa_loaded0"), sem("wa_loaded1")]
        wa_hi_ready = sem("wa_hi_ready")
        wa_lo_ready = sem("wa_lo_ready")
        qk_product = sem("qk_product")
        bias_ready = sem("bias_ready")
        sq_ready = sem("sq_ready")
        qk_out_ready = sem("qk_out_ready")
        acc_ready = sem("acc_ready")
        stored = [sem("stored0"), sem("stored1")]
        col_sums = sem("col_sums")
        rms_ready = sem("rms_ready")
        diag_ready = sem("diag_ready")
        rms_spread = sem("rms_spread")
        rms_row_ready = sem("rms_row_ready")
        y_set = sem("y_set")
        wv_loaded = sem("wv_loaded")
        wo_loaded = sem("wo_loaded")
        wv_hi_ready = sem("wv_hi_ready")
        wv_lo_ready = sem("wv_lo_ready")
        wo_hi_ready = sem("wo_hi_ready")
        wo_lo_ready = sem("wo_lo_ready")
        qk_loaded = [sem(f"qk_loaded{s}") for s in range(4)]
        qk_scaled = sem("qk_scaled")
        qk_hi_ready = sem("qk_hi_ready")
        qk_lo_ready = sem("qk_lo_ready")
        scores_ready = sem("scores_ready")
        max_ready = sem("max_ready")
        exp_ready = sem("exp_ready")
        inv_ready = sem("inv_ready")
        prob_ready = sem("prob_ready")
        pt_product = sem("pt_product")
        pth_ready = sem("pth_ready")
        ptl_ready = sem("ptl_ready")
        v_product = sem("v_product")
        vh_ready = sem("vh_ready")
        vl_ready = sem("vl_ready")
        y_product = sem("y_product")
        o_product = sem("o_product")
        oth_ready = sem("oth_ready")
        otl_ready = sem("otl_ready")
        y_added = sem("y_added")
        ffn_loaded = sem("ffn_loaded")
        ffn_hi_ready = sem("ffn_hi_ready")
        ffn_lo_ready = sem("ffn_lo_ready")
        bb_loaded = sem("bb_loaded")
        x_reloaded = sem("x_reloaded")
        y_normed = sem("y_normed")
        x_added = sem("x_added")
        z_ready = sem("z_ready")
        z_turned = sem("z_turned")
        zh_ready = sem("zh_ready")
        zl_ready = sem("zl_ready")
        hidden_ready = sem("hidden_ready")
        gate_in = sem("gate_in")
        gate_exp = sem("gate_exp")
        hw_ready = sem("hw_ready")
        hw_turned = sem("hw_turned")
        hw_hi_ready = sem("hw_hi_ready")
        hw_lo_ready = sem("hw_lo_ready")
        ffn_product = sem("ffn_product")
        ffn_read = sem("ffn_read")
        ffn_normed = sem("ffn_normed")
        out_ready = [sem("out_ready0"), sem("out_ready1")]
        out_stored = sem("out_stored")

        def f32(ap):
            return ap.bitcast(F32)

        block = ctx.enter_context(nc.Block())

        @block.sync
        def _(sp):
            def load_wa(h, par):
                return sp.dma_start(wa_stage[:, par], w_qk[bass.ds(h, 1)].rearrange(
                    "a p w c n -> p (a w) c n")).then_inc(wa_loaded[par], 16)

            for t in range(TB):
                sp.dma_start(y[:, t, :], x[t]).then_inc(x_loaded[t], 16)
            load_wa(0, 0)
            load_wa(1, 1)
            sp.dma_start(tab[:, :, :], tables).then_inc(tab_loaded, 16)
            for t in range(TB, NT):
                sp.dma_start(y[:, t, :], x[t]).then_inc(x_loaded[t], 16)
            sp.dma_start(wv_stage[:, :, :], w_v[0]).then_inc(wv_loaded, 16)
            sp.dma_start(wo_stage[:, :, :], w_o[0]).then_inc(wo_loaded, 16)
            sp.wait_ge(x_turned, NT)
            for t in range(NT):
                sp.dma_start(y[:, t, :], bo).then_inc(y_set, 16)

            def phase_a(i, first=False, last=False):
                for par in range(2):
                    if not last:
                        sp.wait_ge(wa_lo_ready, 2 * i + par + 1)
                        load_wa(2 * i + 2 + par, par)
                    sp.wait_ge(qk_out_ready, 6 + 2 * par if first else 8 * i + 4 * par + 4)
                    sp.dma_start(q_k_scratch[bass.ds(2 * i + par, 1)].rearrange("a p w n -> p (a w) n"),
                                 qk_out[:, par]).then_inc(stored[par], 16)

            phase_a(0, first=True)
            with sp.Fori(1, PAIRS - 1) as i:
                phase_a(i)
            phase_a(PAIRS - 1, last=True)

            def load_qk(pair, s):
                src = q_k_scratch[bass.ds(2 * pair + s % 2, 1), :, :, (s // 2) * S:(s // 2 + 1) * S]
                sp.dma_start(qk_in[:, s], src.rearrange("a p w n -> p (a w) n")).then_inc(qk_loaded[s], 16)

            sp.wait_ge(stored[0], 16 * PAIRS)
            sp.wait_ge(stored[1], 16 * PAIRS)
            for s in range(4):
                load_qk(0, s)
            sp.wait_ge(wv_lo_ready, 2)
            sp.dma_start(wv_stage[:, :, :], w_v[1]).then_inc(wv_loaded, 16)
            sp.dma_start(wb_stage[:, :, :], w_base).then_inc(ffn_loaded, 16)
            sp.dma_start(in_stage[:, :], w_in).then_inc(ffn_loaded, 16)
            sp.dma_start(bt_stage[:, :], b_t).then_inc(ffn_loaded, 16)
            sp.dma_start(thr_bias[:, :], b_thr).then_inc(ffn_loaded, 16)

            def phase_b(p, last=False):
                for s in range(4):
                    sp.wait_ge(qk_lo_ready, 4 * p + s + 1)
                    load_qk(p + 1, s)
                    if s == 0:
                        sp.wait_ge(wo_lo_ready, 2 * p + 2)
                        sp.dma_start(wo_stage[:, :, :], w_o[bass.ds(p + 1, 1)].rearrange(
                            "a p h n -> p (a h) n")).then_inc(wo_loaded, 16)
                    if s == 2 and not last:
                        sp.wait_ge(wv_lo_ready, 2 * p + 4)
                        sp.dma_start(wv_stage[:, :, :], w_v[bass.ds(p + 2, 1)].rearrange(
                            "a p c n -> p (a c) n")).then_inc(wv_loaded, 16)

            with sp.Fori(0, PAIRS - 2) as p:
                phase_b(p)
            phase_b(PAIRS - 2, last=True)

            sp.wait_ge(qk_lo_ready, 4 * PAIRS)
            for t in range(NT):
                sp.dma_start(x_again[:, t, :], x[t]).then_inc(x_reloaded, 16)
            sp.wait_ge(wv_lo_ready, 2 * PAIRS)
            sp.dma_start(bb, b_base).then_inc(bb_loaded, 16)
            for t in range(NT):
                sp.wait_ge(out_ready[t % 2], t // 2 + 1)
                sp.dma_start(out[t], y[:, t, :]).then_inc(out_stored, 16)
            sp.wait_ge(out_stored, 16 * NT)

        @block.gpsimd
        def _(pool):
            pool.memset(ident[:, :], 0.0).then_inc(const_ready, 1)
            pool.memset(ones[:, :], 1.0).then_inc(const_ready, 1)
            pool.memset(minus_half[:, :], -0.5).then_inc(const_ready, 1)
            pool.wait_ge(const_ready, 3)
            pool.affine_select(out=ident[:, :], in_=ident[:, :], compare_op=ALU.not_equal, fill=1.0,
                               base=0, pattern=[[-1, P]], channel_multiplier=1).then_inc(const_ready, 1)

            roots = [0]

            def inverse_root(dst, src, done):
                roots[0] += 1
                pool.wait_ge(var_ready, roots[0])
                pool.tensor_tensor(dst, src, minus_half[:, 0:src.shape[1]], ALU.pow).then_inc(done, 1)

            def ln_roots(stage, t, k):
                inverse_root(rstd[:, stage, t:t + k], var_eps[:, stage, t:t + k], rstd_ready)

            ln_roots(0, 0, TB)
            for w in range(2):
                pool.memset(acc[:, w, :], 0.0).then_inc(acc_ready, 2)
            ln_roots(0, TB, TB)

            def phase_a(i, first=False):
                for par in range(2):
                    h = 2 * i + par
                    pool.wait_ge(acc_ready, 2 * h + 4)
                    for w in range(2):
                        pool.wait_ge(sq_ready, 5 + 2 * par + w if first else 4 * h + 3 + w)
                        pool.tensor_tensor(acc[:, w, :], acc[:, w, :], squares[:, par, w, :],
                                           ALU.add).then_inc(acc_ready, 1)

            def split_weights(hi_ready, lo_ready, count, lo, stage, hi):
                pool.wait_ge(hi_ready, count)
                pool.tensor_tensor(lo, stage, f32(hi), ALU.subtract).then_inc(lo_ready, 1)

            def split_wv(pair, slot, c):
                split_weights(wv_hi_ready, wv_lo_ready, 2 * pair + c // 2 + 1,
                              wv_lo[:, slot, c:c + 2, :], wv_stage[:, c:c + 2, :], wv_hi[:, slot, c:c + 2, :])

            def split_wo(pair, slot, h):
                split_weights(wo_hi_ready, wo_lo_ready, 2 * pair + h + 1,
                              wo_lo[:, slot, h, :], wo_stage[:, h, :], wo_hi[:, slot, h, :])

            phase_a(0, first=True)
            with pool.Fori(1, PAIRS - 1) as i:
                phase_a(i)
            split_wv(0, 0, 0)
            split_wv(0, 0, 2)
            phase_a(PAIRS - 1)

            for b in range(2):
                cols = slice(NT * b, NT * b + NT)
                inverse_root(rms[:, cols], sq_eps[:, cols], rms_ready)

            def prepare_qk(p, s, m):
                b = s // 2
                pool.wait_ge(qk_loaded[s], 16 * p + 16)
                pool.tensor_tensor(qk_in[:, s], qk_in[:, s], rms_row[:, :, b * S:(b + 1) * S],
                                   ALU.mult).then_inc(qk_scaled, 1)
                pool.wait_ge(qk_hi_ready, m + 1)
                pool.tensor_tensor(qk_lo[:, s % 2], qk_in[:, s], f32(qk_hi[:, s % 2]),
                                   ALU.subtract).then_inc(qk_lo_ready, 1)

            pool.wait_ge(rms_row_ready, 2)
            prepare_qk(0, 0, 0)
            prepare_qk(0, 1, 1)
            pool.wait_ge(rms_row_ready, 4)
            prepare_qk(0, 2, 2)
            split_wo(0, 0, 0)
            split_wo(0, 0, 1)
            prepare_qk(0, 3, 3)
            split_wv(1, 1, 0)
            split_wv(1, 1, 2)

            def pair_steps(p, par, last=False):
                for s in range(4):
                    prepare_qk(p + 1, s, 4 * p + 4 + s)
                    if s < 2:
                        split_wo(p + 1, 1 - par, s)
                    elif not last:
                        split_wv(p + 2, par, 2 * (s - 2))

            with pool.Fori(0, (PAIRS - 2) // 2) as i:
                pair_steps(2 * i, 0)
                pair_steps(2 * i + 1, 1)
            pair_steps(PAIRS - 2, 0, last=True)

            pool.wait_ge(ffn_hi_ready, 3)
            pool.tensor_tensor(wb_lo, wb_stage[:, :, :], f32(wb_hi), ALU.subtract).then_inc(ffn_lo_ready, 1)
            pool.tensor_tensor(in_lo[:, :], in_stage[:, :], f32(in_hi[:, :]), ALU.subtract).then_inc(ffn_lo_ready, 1)
            pool.tensor_tensor(bt_lo, bt_stage[:, :], f32(bt_hi), ALU.subtract).then_inc(ffn_lo_ready, 1)

            def add_x(b):
                for t in range(TB * b, TB * b + TB, 2):
                    pool.wait_ge(y_normed, t + 1)
                    pool.tensor_tensor(y[:, t, :], y[:, t, :], x_again[:, t, :], ALU.add).then_inc(x_added, 1)

            def add_ffn(t):
                pool.wait_ge(ffn_normed, t + 1)
                pool.tensor_tensor(y[:, t, :], y[:, t, :], x_again[:, t, :], ALU.add).then_inc(out_ready[0], 1)

            ln_roots(1, 0, TB)
            pool.wait_ge(x_reloaded, 16 * NT)
            add_x(0)
            ln_roots(2, 0, TB)
            ln_roots(1, TB, TB)
            add_x(1)
            ln_roots(2, TB, TB)
            ln_roots(3, 0, TB)
            add_ffn(0)
            add_ffn(2)
            for t in range(TB, NT):
                ln_roots(3, t, 1)
                if t % 2 == 0:
                    add_ffn(t)

        @block.scalar
        def _(act):
            def split_wa(par, count):
                act.wait_ge(wa_loaded[par], count)
                act.activation(wa_hi[:, par], wa_stage[:, par], ACT.Copy).then_inc(wa_hi_ready, 1)

            def norm_x(b):
                act.wait_ge(nmr_ready, b + 1)
                for t in range(TB * b, TB * b + TB, 2):
                    act.activation(y[:, t, :], y[:, t, :], ACT.Identity, bias=nmr[:, 0, t:t + 1],
                                   scale=rstd[:, 0, t:t + 1]).then_inc(x_normed[0], 1)

            def high_x(b):
                for t in range(TB * b, TB * b + TB):
                    act.wait_ge(x_turned, t + 1)
                    act.activation(xh[:, :, t * P:(t + 1) * P],
                                   ps[:, t, :].rearrange("p (c n) -> p c n", c=C), ACT.Copy).then_inc(xh_ready, 1)

            norm_x(0)
            split_wa(0, 16)
            high_x(0)
            split_wa(1, 16)
            act.wait_ge(tab_loaded, 16)
            norm_x(1)

            def bias_columns(h, par):
                act.activation(q_k_bias[:, par, :], tab[:, 0:2, bass.ds(h, 1)].rearrange(
                    "p w a -> p (w a)"), ACT.Copy).then_inc(bias_ready, 1)

            def square(par, g, count):
                w, b = g % 2, g // 2
                act.wait_ge(qk_product, count)
                act.activation(squares[:, par, w, b * S:(b + 1) * S], ps[:, 4 * par + g, :],
                               ACT.Square, bias=q_k_bias[:, par, w:w + 1]).then_inc(sq_ready, 1)

            bias_columns(0, 0)
            bias_columns(1, 1)
            act.wait_ge(bias_ready, 2)
            for pos, (par, g) in enumerate(FIRST):
                square(par, g, pos + 1)
                if pos == 3:
                    high_x(1)
                if pos == 5:
                    split_wa(0, 32)

            def phase_a(i, last=False):
                for par in range(2):
                    h = 2 * i + par
                    if not (last and par == 1):
                        split_wa(1 - par, 16 * (i + 1 + par))
                    bias_columns(h, par)
                    act.wait_ge(bias_ready, h + 1)
                    act.wait_ge(acc_ready, 2 * h + 2)
                    for g in range(4):
                        square(par, g, 4 * h + g + 1)

            def split_wv(pair, slot, c):
                act.activation(wv_hi[:, slot, c:c + 2, :], wv_stage[:, c:c + 2, :],
                               ACT.Copy).then_inc(wv_hi_ready, 1)

            def split_wo(pair, slot, h):
                act.activation(wo_hi[:, slot, h, :], wo_stage[:, h, :], ACT.Copy).then_inc(wo_hi_ready, 1)

            with act.Fori(1, PAIRS - 1) as i:
                phase_a(i)
            act.wait_ge(wv_loaded, 16)
            split_wv(0, 0, 0)
            split_wv(0, 0, 2)
            phase_a(PAIRS - 1, last=True)

            def evacuate_v(item, tile, bank):
                act.wait_ge(v_product, item)
                act.activation(vh[:, tile:tile + 2, :], ps[:, bank, :].rearrange("p (t n) -> p t n", t=2),
                               ACT.Copy).then_inc(vh_ready, 1)

            def prepare_qk(s, m):
                act.wait_ge(qk_scaled, m + 1)
                act.activation(qk_hi[:, s % 2], qk_in[:, s], ACT.Copy).then_inc(qk_hi_ready, 1)

            evacuate_v(1, 0, 0)
            evacuate_v(2, 2, 1)

            def spread(b):
                for w in range(2):
                    act.wait_ge(rms_spread, 2 * b + w + 1)
                    act.activation(rms_row[:, w, b * S:(b + 1) * S], ps[:, 4 + 2 * b + w, :],
                                   ACT.Copy).then_inc(rms_row_ready, 1)

            spread(0)
            prepare_qk(0, 0)
            evacuate_v(3, 4, 3)
            spread(1)
            evacuate_v(4, 6, 0)
            prepare_qk(1, 1)

            def evacuate_o(s, n):
                act.wait_ge(o_product, n + 1)
                sl, b = s % 2, s // 2
                act.activation(oth[:, sl, b * S:(b + 1) * S], ps[:, WORK + 1, :], ACT.Identity,
                               bias=v_bias[:, sl, :]).then_inc(oth_ready, 1)

            def step(p, s, weights, do_v=True, next_qk=True, first=False):
                n = 4 * p + s
                h, b, sl = 2 * p + s % 2, s // 2, s % 2
                if not first:
                    evacuate_o((s - 1) % 4, n - 1)
                for i in range(TB):
                    act.wait_ge(max_ready, 4 * n + i + 1)
                    act.activation(prob[:, i, :], ps[:, SCORE + i, :], ACT.Exp, bias=neg_max[:, sl, i:i + 1],
                                   accum_out=row_sum[:, sl, i:i + 1]).then_inc(exp_ready, 1)
                for i in range(TB):
                    act.wait_ge(pt_product, 4 * n + i + 1)
                    act.activation(pth[:, :, i * P:(i + 1) * P],
                                   ps[:, TRANS + i % 2, :].rearrange("p (k q) -> p k q", k=TB),
                                   ACT.Copy).then_inc(pth_ready, 1)
                    if i == 1 and do_v:
                        evacuate_v(n + 3, TB * (1 - b) + 2 * sl, WORK)
                if next_qk:
                    prepare_qk((s + 2) % 4, n + 2)
                weights()
                act.activation(v_bias[:, sl, :], tab[:, 4, bass.ds(h, 1)], ACT.Copy).then_inc(bias_ready, 1)
                act.wait_ge(bias_ready, HEADS + n + 1)

            def wo_pair(pair, slot):
                def both():
                    act.wait_ge(wo_loaded, 16 * pair + 16)
                    split_wo(pair, slot, 0)
                    split_wo(pair, slot, 1)
                return both

            def wv_pair(pair, slot):
                def both():
                    act.wait_ge(wv_loaded, 16 * pair + 16)
                    split_wv(pair, slot, 0)
                    split_wv(pair, slot, 2)
                return both

            def wo_part(pair, slot, h):
                def one():
                    act.wait_ge(wo_loaded, 16 * pair + 16)
                    split_wo(pair, slot, h)
                return one

            def wv_part(pair, slot, c):
                def one():
                    act.wait_ge(wv_loaded, 16 * pair + 16)
                    split_wv(pair, slot, c)
                return one

            def nothing():
                pass

            step(0, 0, wo_pair(0, 0), do_v=False, first=True)
            step(0, 1, wv_pair(1, 1), do_v=False)

            def pair_steps(p, par, last=False):
                step(p, 2, wo_part(p + 1, 1 - par, 0))
                step(p, 3, wo_part(p + 1, 1 - par, 1))
                step(p + 1, 0, nothing if last else wv_part(p + 2, par, 0))
                step(p + 1, 1, nothing if last else wv_part(p + 2, par, 2))

            with act.Fori(0, (PAIRS - 2) // 2) as i:
                pair_steps(2 * i, 0)
                pair_steps(2 * i + 1, 1)
            pair_steps(PAIRS - 2, 0, last=True)

            def ffn_weights():
                act.wait_ge(ffn_loaded, 16 * 4)
                act.activation(wb_hi, wb_stage[:, :, :], ACT.Copy).then_inc(ffn_hi_ready, 1)
                act.activation(in_hi[:, :], in_stage[:, :], ACT.Copy).then_inc(ffn_hi_ready, 1)
                act.activation(bt_hi, bt_stage[:, :], ACT.Copy).then_inc(ffn_hi_ready, 1)

            step(PAIRS - 1, 2, ffn_weights, do_v=False, next_qk=False)
            step(PAIRS - 1, 3, nothing, do_v=False, next_qk=False)
            evacuate_o(3, 4 * PAIRS - 1)

            def norm_y(b):
                act.wait_ge(nmr_ready, 3 + b)
                for t in range(TB * b, TB * b + TB):
                    act.activation(y[:, t, :], y[:, t, :], ACT.Identity, bias=nmr[:, 1, t:t + 1],
                                   scale=rstd[:, 1, t:t + 1]).then_inc(y_normed, 1)

            def high_z(b):
                for t in range(TB * b, TB * b + TB):
                    act.wait_ge(z_turned, t + 1)
                    act.activation(xh[:, :, t * P:(t + 1) * P],
                                   ps[:, t, :].rearrange("p (c n) -> p c n", c=C), ACT.Copy).then_inc(zh_ready, 1)

            def gates(b):
                gb = slice(TB * b, TB * b + TB)
                act.wait_ge(gate_in, 2 * b + 1)
                act.activation(g_e[:, gb, :], g_e[:, gb, :], ACT.Exp).then_inc(gate_exp, 1)
                act.wait_ge(gate_in, 2 * b + 2)
                act.activation(g_s[:, 1, gb], g_s[:, 0, gb], ACT.Exp, scale=-1.0).then_inc(gate_exp, 1)
                act.wait_ge(hw_turned, b + 1)
                act.activation(hw_hi[:, b, :], ps[:, HW, :], ACT.Copy).then_inc(hw_hi_ready, 1)

            def norm_ffn(t, count):
                act.wait_ge(nmr_ready, count)
                act.activation(x_again[:, t, :], x_again[:, t, :], ACT.Identity, bias=nmr[:, 3, t:t + 1],
                               scale=rstd[:, 3, t:t + 1]).then_inc(ffn_normed, 1)

            norm_y(0)
            high_z(0)
            norm_y(1)
            gates(0)
            high_z(1)
            for t in range(TB):
                norm_ffn(t, 5)
            gates(1)
            for t in range(TB, NT):
                norm_ffn(t, t + 2)

        @block.tensor
        def _(pe):
            def three(outp, lhs, rhs, first, last):
                pe.matmul(outp, lhs[0], rhs[0], start=first, stop=False)
                pe.matmul(outp, lhs[0], rhs[1], start=False, stop=False)
                return pe.matmul(outp, lhs[1], rhs[0], start=False, stop=last)

            pe.wait_ge(const_ready, 4)

            def turn_x(b):
                for t in range(TB * b, TB * b + TB):
                    pe.wait_ge(x_normed[t % 2], t // 2 + 1)
                    for c in range(C):
                        ins = pe.transpose(ps[:, t, c * P:(c + 1) * P], y[:, t, c * P:(c + 1) * P], ident[:, :])
                    ins.then_inc(x_turned, 1)

            def q_or_k(par, g):
                w, b = g % 2, g // 2
                cols = slice(b * S, (b + 1) * S)
                for c in range(C):
                    ins = three(ps[:, 4 * par + g, :], (wa_hi[:, par, w, c], wa_lo[:, par, w, c]),
                                (xh[:, c, cols], xl[:, c, cols]), c == 0, c == C - 1)
                ins.then_inc(qk_product, 1)

            turn_x(0)
            pe.wait_ge(xl_ready, TB)
            for pos, (par, g) in enumerate(FIRST):
                if pos == 0 or pos == 2:
                    pe.wait_ge(wa_lo_ready, par + 1)
                if pos == 4:
                    pe.wait_ge(qk_out_ready, 4)
                    turn_x(1)
                    pe.wait_ge(xl_ready, NT)
                q_or_k(par, g)

            def phase_a(i):
                for par in range(2):
                    pe.wait_ge(wa_lo_ready, 2 * i + par + 1)
                    for g in range(4):
                        q_or_k(par, g)

            with pe.Fori(1, PAIRS) as i:
                phase_a(i)

            def v_item(slot, tile, bank):
                for k in range(2):
                    cols = slice((tile + k) * P, (tile + k + 1) * P)
                    for c in range(C):
                        ins = three(ps[:, bank, 2 * P * k:2 * P * (k + 1)], (xh[:, c, cols], xl[:, c, cols]),
                                    (wv_hi[:, slot, c], wv_lo[:, slot, c]), c == 0, c == C - 1)
                ins.then_inc(v_product, 1)

            pe.wait_ge(qk_out_ready, 4 * HEADS - 4)
            pe.wait_ge(wv_lo_ready, 2)
            v_item(0, 0, 0)
            v_item(0, 2, 1)
            pe.wait_ge(acc_ready, 4 + 2 * HEADS)
            for b in range(2):
                for w in range(2):
                    for t in range(TB):
                        col = NT * b + TB * w + t
                        tok = slice((TB * b + t) * P, (TB * b + t + 1) * P)
                        ins = pe.matmul(ps[:, 2 + 3 * b, col:col + 1], acc[:, w, tok], ones[:, 0:1],
                                        start=True, stop=True)
                ins.then_inc(col_sums, 1)
                if b == 0:
                    pe.wait_ge(qk_out_ready, 4 * HEADS)

            def spread(b):
                for w in range(2):
                    pe.wait_ge(diag_ready, 2 * b + w + 1)
                    pe.matmul(ps[:, 4 + 2 * b + w, :], ones[:, :], diag[:, 2 * b + w, :],
                              start=True, stop=True).then_inc(rms_spread, 1)

            v_item(0, 4, 3)
            spread(0)
            pe.wait_ge(vl_ready, 1)
            v_item(0, 6, 0)
            spread(1)
            pe.wait_ge(vl_ready, 4)

            def y_item(slot, tile, bank):
                cols = slice(tile * P, (tile + 1) * P)
                for h in range(2):
                    ins = three(ps[:, bank, :], (oth[:, h, cols], otl[:, h, cols]),
                                (wo_hi[:, slot, h, :], wo_lo[:, slot, h, :]), h == 0, h == 1)
                ins.then_inc(y_product, 1)

            def step(p, s, par, do_v=True, y_items=2, first=False):
                n = 4 * p + s
                sl, b = s % 2, s // 2
                pe.wait_ge(qk_lo_ready, n + 1)
                if not first:
                    pe.wait_ge(prob_ready, 4 * n)
                if y_items:
                    pe.wait_ge(y_added, 2 * n - 2)
                for i in range(TB):
                    rows = slice(i * P, (i + 1) * P)
                    three(ps[:, SCORE + i, :], (qk_hi[:, sl, 0, rows], qk_lo[:, sl, 0, rows]),
                          (qk_hi[:, sl, 1, :], qk_lo[:, sl, 1, :]), True, True).then_inc(scores_ready, 1)
                if do_v:
                    pair = p + 1 if b else p
                    pe.wait_ge(wv_lo_ready, 2 * pair + 2)
                    pe.wait_ge(vl_ready, n + 2)
                    v_item(1 - par if b else par, TB * (1 - b) + 2 * sl, WORK)
                y_slot = par if b else 1 - par
                y_tile = (0 if b else TB) + 2 * sl
                for i in range(TB):
                    pe.wait_ge(prob_ready, 4 * n + i + 1)
                    if i >= 2:
                        pe.wait_ge(ptl_ready, 4 * n + i - 1)
                    for k in range(TB):
                        ins = pe.transpose(ps[:, TRANS + i % 2, k * P:(k + 1) * P],
                                           prob[:, i, k * P:(k + 1) * P], ident[:, :])
                    ins.then_inc(pt_product, 1)
                    if i == 1:
                        if not first:
                            pe.wait_ge(otl_ready, n)
                        if y_items:
                            pe.wait_ge(wo_lo_ready, 2 * (p if b else p - 1) + 2)
                            y_item(y_slot, y_tile, SCORE)
                for k in range(1, y_items):
                    y_item(y_slot, y_tile + k, SCORE + k)
                if not first:
                    pe.wait_ge(vl_ready, n + 2 - sl)
                d = slice(sl * P, (sl + 1) * P)
                for half in range(2):
                    pe.wait_ge(ptl_ready, 4 * n + 2 * half + 2)
                    cols = slice(half * 2 * P, (half + 1) * 2 * P)
                    for k in range(TB):
                        ins = three(ps[:, WORK + 1, cols], (vh[:, TB * b + k, d], vl[:, TB * b + k, d]),
                                    (pth[:, k, cols], ptl[:, k, cols]), k == 0, k == TB - 1)
                ins.then_inc(o_product, 1)

            step(0, 0, 0, do_v=False, y_items=0, first=True)
            step(0, 1, 0, do_v=False, y_items=0)

            def pair_steps(p, par):
                step(p, 2, par)
                step(p, 3, par)
                step(p + 1, 0, 1 - par)
                step(p + 1, 1, 1 - par)

            with pe.Fori(0, (PAIRS - 2) // 2) as i:
                pair_steps(2 * i, 0)
                pair_steps(2 * i + 1, 1)
            pair_steps(PAIRS - 2, 0)
            step(PAIRS - 1, 2, 1, do_v=False, y_items=4)
            pe.wait_ge(y_added, 8 * PAIRS - 2)
            step(PAIRS - 1, 3, 1, do_v=False, y_items=0)

            pe.wait_ge(otl_ready, 4 * PAIRS)
            for i in range(TB):
                y_item(1, TB + i, SCORE + i)

            def turn_z(b):
                for t in range(TB * b, TB * b + TB):
                    pe.wait_ge(z_ready, t + 1)
                    for c in range(C):
                        ins = pe.transpose(ps[:, t, c * P:(c + 1) * P],
                                           z[:, t % TB, c * P:(c + 1) * P], ident[:, :])
                    ins.then_inc(z_turned, 1)

            def hidden(b):
                for t in range(TB * b, TB * b + TB):
                    pe.wait_ge(zl_ready, t + 1)
                    if t % 2 == 0 and b:
                        pe.wait_ge(zl_ready, NT)
                    cols = slice(t * P, (t + 1) * P)
                    half = slice(WIDE * (t % 2), WIDE * (t % 2 + 1))
                    for c in range(C):
                        rhs = slice(c * IN, c * IN + WIDE)
                        ins = three(ps[:, HIDDEN + (t % TB) // 2, half], (xh[:, c, cols], xl[:, c, cols]),
                                    (in_hi[:, rhs], in_lo[:, rhs]), c == 0, c == C - 1)
                ins.then_inc(hidden_ready, 1)

            def base(t):
                cols = slice(t * P, (t + 1) * P)
                if t >= TB:
                    pe.wait_ge(ffn_read, t - TB + 1)
                for c in range(C):
                    three(ps[:, t % TB, :], (xh[:, c, cols], xl[:, c, cols]),
                          (wb_hi[:, c, :], wb_lo[:, c, :]), c == 0, False)

            def turn_hw(b):
                pe.wait_ge(hw_ready, b + 1)
                for k in range(TB):
                    ins = pe.transpose(ps[:, HW, k * P:(k + 1) * P], hw[:, b, k * P:(k + 1) * P], ident[:, :])
                ins.then_inc(hw_turned, 1)

            def experts(t):
                b, k = t // TB, t % TB
                pe.wait_ge(hw_lo_ready, b + 1)
                cols = slice(k * P, (k + 1) * P)
                three(ps[:, k, :], (hw_hi[:, b, cols], hw_lo[:, b, cols]), (bt_hi, bt_lo),
                      False, True).then_inc(ffn_product, 1)

            turn_z(0)
            pe.wait_ge(ffn_lo_ready, 3)
            hidden(0)
            for t in range(TB):
                base(t)
            turn_hw(0)
            for t in range(TB):
                experts(t)
            turn_z(1)
            hidden(1)
            base(4)
            base(5)
            turn_hw(1)
            experts(4)
            experts(5)
            for t in (6, 7):
                base(t)
                experts(t)

        @block.vector
        def _(dve):
            links = [0]

            def link(ins):
                links[0] += 1
                ins.then_inc(ln_chain, 1)
                dve.wait_ge(ln_chain, links[0])

            roots = [0]

            def moments(src, stage, t):
                link(dve.bn_stats(stats[:, stage, t, :], src[:, t, :]))
                return dve.bn_aggr(mv[:, stage, t, :], stats[:, stage, t, :])

            def inverse_roots(stage, t, k):
                tiles = slice(t, t + k)
                dve.tensor_scalar(var_eps[:, stage, tiles], mv[:, stage, tiles, 1], LN_EPS, None,
                                  ALU.add).then_inc(var_ready, 1)
                link(dve.tensor_scalar(nmr[:, stage, tiles], mv[:, stage, tiles, 0], -1.0, None, ALU.mult))
                roots[0] += 1
                dve.wait_ge(rstd_ready, roots[0])
                return dve.tensor_tensor(nmr[:, stage, tiles], nmr[:, stage, tiles], rstd[:, stage, tiles],
                                         ALU.mult)

            def low_wa(par):
                dve.tensor_tensor(wa_lo[:, par], wa_stage[:, par], f32(wa_hi[:, par]),
                                  ALU.subtract).then_inc(wa_lo_ready, 1)

            def norm_x(b):
                for t in range(TB * b, TB * b + TB):
                    dve.wait_ge(x_loaded[t], 16)
                    link(moments(y, 0, t))
                inverse_roots(0, TB * b, TB).then_inc(nmr_ready, 1)
                for t in range(TB * b + 1, TB * b + TB, 2):
                    dve.tensor_scalar(y[:, t, :], y[:, t, :], mv[:, 0, t, 0:1], rstd[:, 0, t:t + 1],
                                      ALU.subtract, ALU.mult).then_inc(x_normed[1], 1)

            def low_x(b):
                for t in range(TB * b, TB * b + TB):
                    dve.wait_ge(xh_ready, t + 1)
                    cols = slice(t * P, (t + 1) * P)
                    dve.tensor_tensor(xl[:, :, cols], ps[:, t, :].rearrange("p (c n) -> p c n", c=C),
                                      f32(xh[:, :, cols]), ALU.subtract).then_inc(xl_ready, 1)

            norm_x(0)
            dve.wait_ge(wa_hi_ready, 1)
            low_wa(0)
            low_x(0)
            dve.wait_ge(wa_hi_ready, 2)
            low_wa(1)
            norm_x(1)
            dve.wait_ge(tab_loaded, 16)

            def store_qk(par, g, h, count):
                w, b = g % 2, g // 2
                dve.wait_ge(sq_ready, count)
                dve.tensor_scalar(qk_out[:, par, w, b * S:(b + 1) * S], ps[:, 4 * par + g, :],
                                  tab[:, w, bass.ds(h, 1)], tab[:, 2 + w, bass.ds(h, 1)],
                                  ALU.add, ALU.mult).then_inc(qk_out_ready, 1)

            for pos, (par, g) in enumerate(FIRST):
                store_qk(par, g, par, pos + 1)
                if pos == 3:
                    low_x(1)
                if pos == 5:
                    dve.wait_ge(wa_hi_ready, 3)
                    low_wa(0)

            def phase_a(i, last=False):
                for par in range(2):
                    h = 2 * i + par
                    if not (last and par == 1):
                        dve.wait_ge(wa_hi_ready, h + 2)
                        low_wa(1 - par)
                    dve.wait_ge(stored[par], 16 * i)
                    for g in range(4):
                        store_qk(par, g, h, 4 * h + g + 1)

            with dve.Fori(1, PAIRS - 1) as i:
                phase_a(i)
            phase_a(PAIRS - 1, last=True)

            def split_v(item, tile, bank):
                dve.wait_ge(vh_ready, item)
                dve.tensor_tensor(vl[:, tile:tile + 2, :], ps[:, bank, :].rearrange("p (t n) -> p t n", t=2),
                                  f32(vh[:, tile:tile + 2, :]), ALU.subtract).then_inc(vl_ready, 1)

            split_v(1, 0, 0)
            split_v(2, 2, 1)
            for b in range(2):
                cols = slice(NT * b, NT * b + NT)
                dve.wait_ge(col_sums, b + 1)
                dve.tensor_scalar(sq_eps[:, cols], ps[:, 2 + 3 * b, cols], 1.0 / INNER, RMS_EPS,
                                  ALU.mult, ALU.add).then_inc(var_ready, 1)
            for b in range(2):
                dve.wait_ge(rms_ready, b + 1)
                for w in range(2):
                    for k in range(TB):
                        col = NT * b + TB * w + k
                        ins = dve.tensor_scalar(diag[:, 2 * b + w, k * P:(k + 1) * P], ident[:, :],
                                                rms[:, col:col + 1], 1.0 if w else SCORE_SCALE,
                                                ALU.mult, ALU.mult)
                    ins.then_inc(diag_ready, 1)
            split_v(3, 4, 3)
            split_v(4, 6, 0)
            dve.wait_ge(y_set, 16 * NT)
            dve.sem_inc(y_added, 2)

            def add_y(count, tile, bank):
                dve.wait_ge(y_product, count)
                return dve.tensor_tensor(y[:, tile, :], y[:, tile, :], ps[:, bank, :], ALU.add)

            def evacuate_o(h, s, n):
                sl, b = s % 2, s // 2
                cols = slice(b * S, (b + 1) * S)
                dve.wait_ge(oth_ready, n + 1)
                dve.scalar_tensor_tensor(out=otl[:, sl, cols], in0=ps[:, WORK + 1, :],
                                         scalar=tab[:, 4, bass.ds(h, 1)], in1=f32(oth[:, sl, cols]),
                                         op0=ALU.add, op1=ALU.subtract).then_inc(otl_ready, 1)

            def step(p, s, do_v=True, y_items=2, first=False):
                n = 4 * p + s
                b, sl = s // 2, s % 2
                for i in range(TB):
                    dve.wait_ge(scores_ready, 4 * n + i + 1)
                    dve.tensor_reduce(neg_max[:, sl, i:i + 1], ps[:, SCORE + i, :], AX.X, ALU.max,
                                      negate=True).then_inc(max_ready, 1)
                    if i == 1 and not first:
                        evacuate_o(2 * p + 1 - sl if s else 2 * p - 1, (s - 1) % 4, n - 1)
                for i in range(TB):
                    dve.wait_ge(exp_ready, 4 * n + i + 1)
                    dve.reciprocal(row_inv[:, sl, i:i + 1], row_sum[:, sl, i:i + 1]).then_inc(inv_ready, 1)
                    dve.wait_ge(inv_ready, 4 * n + i + 1)
                    dve.tensor_scalar(prob[:, i, :], prob[:, i, :], row_inv[:, sl, i:i + 1], None,
                                      ALU.mult).then_inc(prob_ready, 1)
                for i in range(TB):
                    dve.wait_ge(pth_ready, 4 * n + i + 1)
                    rows = slice(i * P, (i + 1) * P)
                    dve.tensor_tensor(ptl[:, :, rows], ps[:, TRANS + i % 2, :].rearrange("p (k q) -> p k q", k=TB),
                                      f32(pth[:, :, rows]), ALU.subtract).then_inc(ptl_ready, 1)
                    if i == 1 and do_v:
                        split_v(n + 3, TB * (1 - b) + 2 * sl, WORK)
                for k in range(y_items):
                    add_y(2 * n - 3 + k, (0 if b else TB) + 2 * sl + k, SCORE + k).then_inc(y_added, 1)

            step(0, 0, do_v=False, y_items=0, first=True)
            step(0, 1, do_v=False, y_items=0)

            def pair_steps(p):
                step(p, 2)
                step(p, 3)
                step(p + 1, 0)
                step(p + 1, 1)

            with dve.Fori(0, (PAIRS - 2) // 2) as i:
                pair_steps(2 * i)
                pair_steps(2 * i + 1)
            pair_steps(PAIRS - 2)
            step(PAIRS - 1, 2, do_v=False, y_items=4)
            step(PAIRS - 1, 3, do_v=False, y_items=0)

            def final_y(b):
                for t in range(TB * b, TB * b + TB):
                    link(moments(y, 1, t))
                    if t == 2:
                        evacuate_o(HEADS - 1, 3, 4 * PAIRS - 1)
                inverse_roots(1, TB * b, TB).then_inc(nmr_ready, 1)

            def make_z(b):
                for t in range(TB * b, TB * b + TB):
                    if t % 2:
                        dve.wait_ge(y_normed, t + 1)
                        link(dve.tensor_tensor(y[:, t, :], y[:, t, :], x_again[:, t, :], ALU.add))
                    else:
                        dve.wait_ge(x_added, t // 2 + 1)
                    link(moments(y, 2, t))
                inverse_roots(2, TB * b, TB)
                for t in range(TB * b, TB * b + TB):
                    if b:
                        dve.wait_ge(z_turned, t - TB + 1)
                    dve.tensor_scalar(z[:, t % TB, :], y[:, t, :], mv[:, 2, t, 0:1], rstd[:, 2, t:t + 1],
                                      ALU.subtract, ALU.mult).then_inc(z_ready, 1)
                for t in range(TB * b, TB * b + TB):
                    dve.wait_ge(zh_ready, t + 1)
                    cols = slice(t * P, (t + 1) * P)
                    dve.tensor_tensor(xl[:, :, cols], ps[:, t, :].rearrange("p (c n) -> p c n", c=C),
                                      f32(xh[:, :, cols]), ALU.subtract).then_inc(zl_ready, 1)

            def gates(b):
                gb = slice(TB * b, TB * b + TB)
                both = ps[:, HIDDEN:HIDDEN + 2, :].rearrange("p j (i n) -> p (j i) n", n=WIDE)

                def over_experts(k):
                    return g_s[:, k, gb].unsqueeze(2).broadcast_to([P, TB, E])

                dve.wait_ge(hidden_ready, b + 1)
                link(dve.tensor_reduce(g_s[:, 2, gb], both[:, :, P:P + E], AX.X, ALU.max))
                dve.tensor_tensor(g_e[:, gb, :], both[:, :, P:P + E], over_experts(2),
                                  ALU.subtract).then_inc(gate_in, 1)
                dve.tensor_scalar(g_s[:, 0, gb], both[:, :, P + E], thr_bias[:, 0:1], None,
                                  ALU.add).then_inc(gate_in, 1)
                dve.wait_ge(gate_exp, 2 * b + 2)
                link(dve.tensor_reduce(g_s[:, 3, gb], g_e[:, gb, :], AX.X, ALU.add))
                link(dve.reciprocal(g_s[:, 4, gb], g_s[:, 3, gb]))
                link(dve.tensor_scalar(g_s[:, 5, gb], g_s[:, 1, gb], 8.0, 8.0, ALU.mult, ALU.add))
                link(dve.reciprocal(g_s[:, 6, gb], g_s[:, 5, gb]))
                link(dve.tensor_tensor(g_p[:, gb, :], g_e[:, gb, :], over_experts(4), ALU.mult))
                link(dve.tensor_tensor(g_w[:, gb, :], g_p[:, gb, :], over_experts(6), ALU.subtract))
                link(dve.tensor_scalar(g_p[:, gb, :], g_w[:, gb, :], 0.0, 2.0, ALU.max, ALU.mult))
                link(dve.tensor_reduce(g_s[:, 7, gb], g_p[:, gb, :], AX.X, ALU.add))
                link(dve.tensor_scalar(g_s[:, 8, gb], g_s[:, 7, gb], 0.0, None, ALU.is_equal))
                link(dve.scalar_tensor_tensor(out=g_s[:, 9, gb], in0=g_s[:, 7, gb], scalar=0.5,
                                              in1=g_s[:, 8, gb], op0=ALU.mult, op1=ALU.add))
                link(dve.reciprocal(g_s[:, 7, gb], g_s[:, 9, gb]))
                link(dve.tensor_tensor(g_w[:, gb, :], g_p[:, gb, :], over_experts(7), ALU.mult))
                dve.tensor_tensor(hw[:, b, :].rearrange("p (t e r) -> p t e r", e=E, r=R),
                                  both[:, :, 0:P].rearrange("p t (e r) -> p t e r", r=R),
                                  g_w[:, gb, :].unsqueeze(3).broadcast_to([P, TB, E, R]),
                                  ALU.mult).then_inc(hw_ready, 1)
                dve.wait_ge(hw_hi_ready, b + 1)
                dve.tensor_tensor(hw_lo[:, b, :], ps[:, HW, :], f32(hw_hi[:, b, :]),
                                  ALU.subtract).then_inc(hw_lo_ready, 1)

            def add_bias(t):
                dve.wait_ge(ffn_product, t + 1)
                return dve.tensor_tensor(x_again[:, t, :], ps[:, t % TB, :], bb, ALU.add)

            def add_ffn(t):
                dve.wait_ge(ffn_normed, t + 1)
                dve.tensor_tensor(y[:, t, :], y[:, t, :], x_again[:, t, :], ALU.add).then_inc(out_ready[1], 1)

            final_y(0)
            done = 8 * PAIRS - 4
            for t in range(TB, NT):
                link(add_y(done + t - TB + 1, t, SCORE + t - TB))
            make_z(0)
            final_y(1)
            gates(0)
            make_z(1)
            dve.wait_ge(bb_loaded, 16)
            for t in range(TB):
                add_bias(t).then_inc(ffn_read, 1)
            dve.wait_ge(ffn_read, TB)
            for t in range(TB):
                link(moments(x_again, 3, t))
            inverse_roots(3, 0, TB).then_inc(nmr_ready, 1)
            gates(1)
            add_ffn(1)
            add_ffn(3)
            for t in range(TB, NT):
                link(add_bias(t))
                link(moments(x_again, 3, t))
                inverse_roots(3, t, 1).then_inc(nmr_ready, 1)
                if t % 2:
                    add_ffn(t)


def kernel(L0_attn_hidden_states, L0_attn_Wq, L0_attn_bq, L0_attn_Wk, L0_attn_bk, L0_attn_Wv, L0_attn_bv,
           L0_attn_Wo, L0_attn_bo, L0_attn_gq, L0_attn_gk, L0_ffn_W_base, L0_ffn_b_base, L0_ffn_W_gate,
           L0_ffn_W_thr, L0_ffn_b_thr, L0_ffn_A, L0_ffn_B):
    import numpy as np
    import concourse.bacc as bacc
    from concourse.bass_utils import run_bass_kernel_spmd

    x = np.asarray(L0_attn_hidden_states)
    D, C = x.shape[-1], x.shape[-1] // P
    inner = L0_attn_Wq.shape[1]
    heads = inner // P

    def by_head(w, n):
        return np.asarray(w).reshape(C, P, inner // n, n).transpose(2, 1, 0, 3)

    def chunks(w):
        return np.asarray(w).reshape(C, P, -1).transpose(1, 0, 2)

    def columns(v):
        return np.asarray(v).reshape(heads, P).T

    def on_all(v):
        return np.broadcast_to(np.asarray(v), (P, v.shape[0]))

    gate = np.concatenate([np.asarray(L0_ffn_W_gate), np.asarray(L0_ffn_W_thr)])
    a_gate = chunks(np.concatenate([np.asarray(L0_ffn_A).reshape(-1, D), gate]).T)
    pad = 2 * P - a_gate.shape[2]
    a_gate = np.concatenate([a_gate.reshape(P, -1), np.zeros((P, pad), a_gate.dtype)], axis=1)
    arrays = {
        "x": x.reshape(-1, P, D),
        "w_qk": np.stack([by_head(L0_attn_Wq, P), by_head(L0_attn_Wk, P)], axis=2),
        "w_v": by_head(L0_attn_Wv, 2 * P),
        "w_o": np.asarray(L0_attn_Wo).reshape(heads // 2, 2, P, D).transpose(0, 2, 1, 3),
        "tables": np.stack([columns(v) for v in (L0_attn_bq, L0_attn_bk, L0_attn_gq, L0_attn_gk, L0_attn_bv)],
                           axis=1),
        "bo": on_all(L0_attn_bo),
        "w_base": chunks(np.asarray(L0_ffn_W_base).T),
        "w_in": a_gate,
        "b_t": np.asarray(L0_ffn_B).transpose(0, 2, 1).reshape(P, -1),
        "b_base": on_all(L0_ffn_b_base),
        "b_thr": on_all(L0_ffn_b_thr),
    }
    nc = bacc.Bacc("TRN2", target_bir_lowering=False, num_devices=1)
    arrays = {name: np.ascontiguousarray(a) for name, a in arrays.items()}
    aps = [nc.dram_tensor(name, a.shape, mybir.dt.from_np(a.dtype), kind="ExternalInput").ap()
           for name, a in arrays.items()]
    out = nc.dram_tensor("out", arrays["x"].shape, F32, kind="ExternalOutput").ap()
    build(nc, *aps, out)
    r = run_bass_kernel_spmd(nc, [arrays], core_ids=[0])
    return r.results[0]["out"].reshape(x.shape)
```

```python
from contextlib import ExitStack

import concourse.bass as bass
from concourse import mybir

F32 = mybir.dt.float32
F32R = mybir.dt.float32r
ALU = mybir.AluOpType
ACT = mybir.ActivationFunctionType
AX = mybir.AxisListType

P = 128


def build(nc, x, w_qk, w_v, w_o, tables, bo, w_base, w_in, b_t, b_base, b_thr, out):
    NT = x.shape[0]
    D = x.shape[2]
    C = D // P
    HEADS = w_qk.shape[0]
    INNER = HEADS * P
    PAIRS = HEADS // 2
    TB = NT // 2
    S = TB * P
    TOK = NT * P
    E = 8
    R = P // E
    IN = P + E + 1
    WIDE = 2 * P
    LN_EPS, RMS_EPS = 1e-5, 1e-6
    SCORE_SCALE = float(P) ** -0.5
    assert C == TB == 4 and S == 512

    FIRST = [(par, g) for b in range(2) for par in range(2) for g in (2 * b, 2 * b + 1)]

    q_k_scratch = nc.dram_tensor("q_k_scratch", [HEADS, P, 2, TOK], F32, kind="Internal").ap()

    with ExitStack() as ctx:
        def sb(name, shape, dt=F32, stack=ctx):
            return stack.enter_context(nc.sbuf_tensor(name, shape, dt))

        def sem(name):
            return ctx.enter_context(nc.semaphore(name))

        ps = ctx.enter_context(nc.psum_tensor("ps", [P, 8, 512], F32))
        SCORE, TRANS, WORK = 0, 4, 6

        Z = ((4, 5, 6, 7), (7, 2, 3, 6))
        HIDDEN = (2, 0)
        BASE = ((0, 1, 4, 5), (4, 5, 6, 7))
        HW = (6, 2)

        y = sb("y", [P, NT, D])
        xh = sb("xh", [P, C, TOK], F32R)
        xl = sb("xl", [P, C, TOK], F32R)
        ident = sb("ident", [P, P])
        ones = sb("ones", [P, P])
        tab = sb("tab", [P, 5, HEADS])
        wv_stage = sb("wv_stage", [P, C, 2 * P])
        wv_hi = sb("wv_hi", [P, 2, C, 2 * P], F32R)
        wv_lo = sb("wv_lo", [P, 2, C, 2 * P], F32R)
        wo_stage = sb("wo_stage", [P, 2, D])
        wb_stage = sb("wb_stage", [P, C, D])
        in_stage = sb("in_stage", [P, w_in.shape[1]])
        in_hi = sb("in_hi", [P, w_in.shape[1]], F32R)
        in_lo = sb("in_lo", [P, w_in.shape[1]], F32R)
        bt_stage = sb("bt_stage", [P, D])
        thr_bias = sb("thr_bias", [P, 1])
        stats = sb("stats", [P, 4, NT, 6])
        mv = sb("mv", [P, 4, NT, 2])
        var_eps = sb("var_eps", [P, 4, NT])
        rstd = sb("rstd", [P, 4, NT])
        nmr = sb("nmr", [P, 4, NT])
        sq_eps = sb("sq_eps", [P, 2 * NT])
        q_k_bias = sb("q_k_bias", [P, 2, 2])
        v_bias = sb("v_bias", [P, 2, 1])
        minus_half = sb("minus_half", [P, 2 * NT])
        rms = sb("rms", [P, 2 * NT])
        neg_max = sb("neg_max", [P, 2, TB])
        row_sum = sb("row_sum", [P, 2, TB])
        row_inv = sb("row_inv", [P, 2, TB])

        with ExitStack() as a_only:
            wa_stage = sb("wa_stage", [P, 2, 2, C, P], F32, a_only)
            wa_hi = sb("wa_hi", [P, 2, 2, C, P], F32R, a_only)
            wa_lo = sb("wa_lo", [P, 2, 2, C, P], F32R, a_only)
            qk_out = sb("qk_out", [P, 2, 2, TOK], F32, a_only)
            squares = sb("squares", [P, 2, 2, TOK], F32, a_only)
            acc = sb("acc", [P, 2, TOK], F32, a_only)

        vh = sb("vh", [P, NT, 2 * P], F32R)
        vl = sb("vl", [P, NT, 2 * P], F32R)
        oth = sb("oth", [P, 2, TOK], F32R)
        otl = sb("otl", [P, 2, TOK], F32R)
        pth = sb("pth", [P, TB, S], F32R)
        ptl = sb("ptl", [P, TB, S], F32R)
        wo_hi = sb("wo_hi", [P, 2, 2, D], F32R)
        wo_lo = sb("wo_lo", [P, 2, 2, D], F32R)
        qk_in = sb("qk_in", [P, 4, 2, S])
        qk_hi = sb("qk_hi", [P, 2, 2, S], F32R)
        qk_lo = sb("qk_lo", [P, 2, 2, S], F32R)
        rms_row = sb("rms_row", [P, 2, TOK])
        prob = sb("prob", [P, TB, S])

        diag = prob

        wb_hi = wv_hi[:, :, :, :].rearrange("p a c n -> p (a c n)").rearrange("p (c n) -> p c n", c=C)
        wb_lo = wv_lo[:, :, :, :].rearrange("p a c n -> p (a c n)").rearrange("p (c n) -> p c n", c=C)
        bt_hi, bt_lo = wo_hi[:, 0, 0, :], wo_lo[:, 0, 0, :]
        x_again = qk_in[:, :, :, :].rearrange("p a w n -> p (a w) n")
        z = prob
        hw = rms_row[:, 0, :].rearrange("p (b n) -> p b n", b=2)
        hw_hi, hw_lo = pth, ptl
        bb = wv_stage[:, 0:2, :].rearrange("p a n -> p (a n)")
        g_e = sb("g_e", [P, NT, E])
        g_p = sb("g_p", [P, NT, E])
        g_w = sb("g_w", [P, NT, E])
        g_s = sb("g_s", [P, 10, NT])

        x_loaded = [sem(f"x_loaded{t}") for t in range(NT)]
        tab_loaded = sem("tab_loaded")
        const_ready = sem("const_ready")
        stats_ready = sem("stats_ready")
        mv_ready = sem("mv_ready")
        chain = sem("chain")
        nmr_ready = sem("nmr_ready")
        var_ready = sem("var_ready")
        rstd_ready = sem("rstd_ready")
        x_normed = [sem("x_normed0"), sem("x_normed1")]
        x_turned = sem("x_turned")
        xh_ready = sem("xh_ready")
        xl_ready = sem("xl_ready")
        wa_loaded = [sem("wa_loaded0"), sem("wa_loaded1")]
        wa_hi_ready = sem("wa_hi_ready")
        wa_lo_ready = sem("wa_lo_ready")
        qk_product = sem("qk_product")
        bias_ready = sem("bias_ready")
        sq_ready = sem("sq_ready")
        qk_out_ready = sem("qk_out_ready")
        acc_ready = sem("acc_ready")
        stored = [sem("stored0"), sem("stored1")]
        col_sums = sem("col_sums")
        rms_ready = sem("rms_ready")
        diag_ready = sem("diag_ready")
        rms_spread = sem("rms_spread")
        rms_row_ready = sem("rms_row_ready")
        y_set = sem("y_set")
        wv_loaded = sem("wv_loaded")
        wo_loaded = sem("wo_loaded")
        wv_hi_ready = sem("wv_hi_ready")
        wv_lo_ready = sem("wv_lo_ready")
        wo_hi_ready = sem("wo_hi_ready")
        wo_lo_ready = sem("wo_lo_ready")
        qk_loaded = [sem(f"qk_loaded{s}") for s in range(4)]
        qk_scaled = sem("qk_scaled")
        qk_hi_ready = sem("qk_hi_ready")
        qk_lo_ready = sem("qk_lo_ready")
        scores_ready = sem("scores_ready")
        max_ready = sem("max_ready")
        exp_ready = sem("exp_ready")
        inv_ready = sem("inv_ready")
        prob_ready = sem("prob_ready")
        pt_product = sem("pt_product")
        pth_ready = sem("pth_ready")
        ptl_ready = sem("ptl_ready")
        v_product = sem("v_product")
        vh_ready = sem("vh_ready")
        vl_ready = sem("vl_ready")
        y_product = sem("y_product")
        o_product = sem("o_product")
        oth_ready = sem("oth_ready")
        otl_ready = sem("otl_ready")
        y_added = sem("y_added")
        ffn_loaded = sem("ffn_loaded")
        ffn_hi_ready = sem("ffn_hi_ready")
        ffn_lo_ready = sem("ffn_lo_ready")
        bb_loaded = sem("bb_loaded")
        x_reloaded = sem("x_reloaded")
        y_normed = sem("y_normed")
        x_added = sem("x_added")
        z_ready = [sem("z_ready0"), sem("z_ready1")]
        z_turned = sem("z_turned")
        zh_ready = sem("zh_ready")
        zl_ready = sem("zl_ready")
        hidden_ready = sem("hidden_ready")
        gate_in = sem("gate_in")
        gate_exp = sem("gate_exp")
        hw_ready = sem("hw_ready")
        hw_turned = sem("hw_turned")
        hw_hi_ready = sem("hw_hi_ready")
        hw_lo_ready = sem("hw_lo_ready")
        ffn_product = sem("ffn_product")
        ffn_read = sem("ffn_read")
        ffn_normed = sem("ffn_normed")
        out_ready = [sem("out_ready0"), sem("out_ready1")]
        out_stored = sem("out_stored")

        def f32(ap):
            return ap.bitcast(F32)

        block = ctx.enter_context(nc.Block())

        @block.sync
        def _(sp):
            def load_wa(h, par):
                return sp.dma_start(wa_stage[:, par], w_qk[bass.ds(h, 1)].rearrange(
                    "a p w c n -> p (a w) c n")).then_inc(wa_loaded[par], 16)

            for t in range(TB):
                sp.dma_start(y[:, t, :], x[t]).then_inc(x_loaded[t], 16)
            load_wa(0, 0)
            load_wa(1, 1)
            sp.dma_start(tab[:, :, :], tables).then_inc(tab_loaded, 16)
            for t in range(TB, NT):
                sp.dma_start(y[:, t, :], x[t]).then_inc(x_loaded[t], 16)
            sp.dma_start(wv_stage[:, :, :], w_v[0]).then_inc(wv_loaded, 16)
            sp.dma_start(wo_stage[:, :, :], w_o[0]).then_inc(wo_loaded, 16)
            sp.wait_ge(x_turned, NT)
            for t in range(NT):
                sp.dma_start(y[:, t, :], bo).then_inc(y_set, 16)

            def phase_a(i, first=False, last=False):
                for par in range(2):
                    if not last:
                        sp.wait_ge(wa_lo_ready, 2 * i + par + 1)
                        load_wa(2 * i + 2 + par, par)
                    sp.wait_ge(qk_out_ready, 6 + 2 * par if first else 8 * i + 4 * par + 4)
                    sp.dma_start(q_k_scratch[bass.ds(2 * i + par, 1)].rearrange("a p w n -> p (a w) n"),
                                 qk_out[:, par]).then_inc(stored[par], 16)

            phase_a(0, first=True)
            with sp.Fori(1, PAIRS - 1) as i:
                phase_a(i)
            phase_a(PAIRS - 1, last=True)

            def load_qk(pair, s):
                src = q_k_scratch[bass.ds(2 * pair + s % 2, 1), :, :, (s // 2) * S:(s // 2 + 1) * S]
                sp.dma_start(qk_in[:, s], src.rearrange("a p w n -> p (a w) n")).then_inc(qk_loaded[s], 16)

            sp.wait_ge(stored[0], 16 * PAIRS)
            sp.wait_ge(stored[1], 16 * PAIRS)
            for s in range(4):
                load_qk(0, s)
            sp.wait_ge(wv_lo_ready, 2)
            sp.dma_start(wv_stage[:, :, :], w_v[1]).then_inc(wv_loaded, 16)
            sp.dma_start(wb_stage[:, :, :], w_base).then_inc(ffn_loaded, 16)
            sp.dma_start(in_stage[:, :], w_in).then_inc(ffn_loaded, 16)
            sp.dma_start(bt_stage[:, :], b_t).then_inc(ffn_loaded, 16)
            sp.dma_start(thr_bias[:, :], b_thr).then_inc(ffn_loaded, 16)

            def phase_b(p, last=False):
                for s in range(4):
                    sp.wait_ge(qk_lo_ready, 4 * p + s + 1)
                    load_qk(p + 1, s)
                    if s == 0:
                        sp.wait_ge(wo_lo_ready, 2 * p + 2)
                        sp.dma_start(wo_stage[:, :, :], w_o[bass.ds(p + 1, 1)].rearrange(
                            "a p h n -> p (a h) n")).then_inc(wo_loaded, 16)
                    if s == 2 and not last:
                        sp.wait_ge(wv_lo_ready, 2 * p + 4)
                        sp.dma_start(wv_stage[:, :, :], w_v[bass.ds(p + 2, 1)].rearrange(
                            "a p c n -> p (a c) n")).then_inc(wv_loaded, 16)

            with sp.Fori(0, PAIRS - 2) as p:
                phase_b(p)
            phase_b(PAIRS - 2, last=True)

            sp.wait_ge(qk_lo_ready, 4 * PAIRS)
            for t in range(NT):
                sp.dma_start(x_again[:, t, :], x[t]).then_inc(x_reloaded, 16)
            sp.wait_ge(wv_lo_ready, 2 * PAIRS)
            sp.dma_start(bb, b_base).then_inc(bb_loaded, 16)
            for t in range(NT):
                sp.wait_ge(out_ready[t % 2], t // 2 + 1)
                sp.dma_start(out[t], y[:, t, :]).then_inc(out_stored, 16)
            sp.wait_ge(out_stored, 16 * NT)

        @block.gpsimd
        def _(pool):
            pool.memset(ident[:, :], 0.0).then_inc(const_ready, 1)
            pool.memset(ones[:, :], 1.0).then_inc(const_ready, 1)
            pool.memset(minus_half[:, :], -0.5).then_inc(const_ready, 1)
            pool.wait_ge(const_ready, 3)
            pool.affine_select(out=ident[:, :], in_=ident[:, :], compare_op=ALU.not_equal, fill=1.0,
                               base=0, pattern=[[-1, P]], channel_multiplier=1).then_inc(const_ready, 1)

            roots = [0]

            def inverse_root(dst, src, done):
                roots[0] += 1
                pool.wait_ge(var_ready, roots[0])
                pool.tensor_tensor(dst, src, minus_half[:, 0:src.shape[1]], ALU.pow).then_inc(done, 1)

            def ln_roots(stage, t, k):
                inverse_root(rstd[:, stage, t:t + k], var_eps[:, stage, t:t + k], rstd_ready)

            ln_roots(0, 0, TB)
            for w in range(2):
                pool.memset(acc[:, w, :], 0.0).then_inc(acc_ready, 2)
            ln_roots(0, TB, TB)

            def phase_a(i, first=False):
                for par in range(2):
                    h = 2 * i + par
                    pool.wait_ge(acc_ready, 2 * h + 4)
                    for w in range(2):
                        pool.wait_ge(sq_ready, 5 + 2 * par + w if first else 4 * h + 3 + w)
                        pool.tensor_tensor(acc[:, w, :], acc[:, w, :], squares[:, par, w, :],
                                           ALU.add).then_inc(acc_ready, 1)

            def split_weights(hi_ready, lo_ready, count, lo, stage, hi):
                pool.wait_ge(hi_ready, count)
                pool.tensor_tensor(lo, stage, f32(hi), ALU.subtract).then_inc(lo_ready, 1)

            def split_wv(pair, slot, c):
                split_weights(wv_hi_ready, wv_lo_ready, 2 * pair + c // 2 + 1,
                              wv_lo[:, slot, c:c + 2, :], wv_stage[:, c:c + 2, :], wv_hi[:, slot, c:c + 2, :])

            def split_wo(pair, slot, h):
                split_weights(wo_hi_ready, wo_lo_ready, 2 * pair + h + 1,
                              wo_lo[:, slot, h, :], wo_stage[:, h, :], wo_hi[:, slot, h, :])

            phase_a(0, first=True)
            with pool.Fori(1, PAIRS - 1) as i:
                phase_a(i)
            split_wv(0, 0, 0)
            split_wv(0, 0, 2)
            phase_a(PAIRS - 1)

            for b in range(2):
                cols = slice(NT * b, NT * b + NT)
                inverse_root(rms[:, cols], sq_eps[:, cols], rms_ready)

            def prepare_qk(p, s, m):
                b = s // 2
                pool.wait_ge(qk_loaded[s], 16 * p + 16)
                pool.tensor_tensor(qk_in[:, s], qk_in[:, s], rms_row[:, :, b * S:(b + 1) * S],
                                   ALU.mult).then_inc(qk_scaled, 1)
                pool.wait_ge(qk_hi_ready, m + 1)
                pool.tensor_tensor(qk_lo[:, s % 2], qk_in[:, s], f32(qk_hi[:, s % 2]),
                                   ALU.subtract).then_inc(qk_lo_ready, 1)

            pool.wait_ge(rms_row_ready, 2)
            prepare_qk(0, 0, 0)
            prepare_qk(0, 1, 1)
            pool.wait_ge(rms_row_ready, 4)
            prepare_qk(0, 2, 2)
            split_wo(0, 0, 0)
            split_wo(0, 0, 1)
            prepare_qk(0, 3, 3)
            split_wv(1, 1, 0)
            split_wv(1, 1, 2)

            def pair_steps(p, par, last=False):
                for s in range(4):
                    prepare_qk(p + 1, s, 4 * p + 4 + s)
                    if s < 2:
                        split_wo(p + 1, 1 - par, s)
                    elif not last:
                        split_wv(p + 2, par, 2 * (s - 2))

            with pool.Fori(0, (PAIRS - 2) // 2) as i:
                pair_steps(2 * i, 0)
                pair_steps(2 * i + 1, 1)
            pair_steps(PAIRS - 2, 0, last=True)

            pool.wait_ge(ffn_hi_ready, 3)
            pool.tensor_tensor(wb_lo, wb_stage[:, :, :], f32(wb_hi), ALU.subtract).then_inc(ffn_lo_ready, 1)
            pool.tensor_tensor(in_lo[:, :], in_stage[:, :], f32(in_hi[:, :]), ALU.subtract).then_inc(ffn_lo_ready, 1)
            pool.tensor_tensor(bt_lo, bt_stage[:, :], f32(bt_hi), ALU.subtract).then_inc(ffn_lo_ready, 1)

            def add_x(b):
                for t in range(TB * b, TB * b + TB, 2):
                    pool.wait_ge(y_normed, t + 1)
                    pool.tensor_tensor(y[:, t, :], y[:, t, :], x_again[:, t, :], ALU.add).then_inc(x_added, 1)

            def add_ffn(t):
                pool.wait_ge(ffn_normed, t + 1)
                pool.tensor_tensor(y[:, t, :], y[:, t, :], x_again[:, t, :], ALU.add).then_inc(out_ready[0], 1)

            ln_roots(1, 0, TB)
            pool.wait_ge(x_reloaded, 16 * NT)
            add_x(0)
            ln_roots(2, 0, TB)
            ln_roots(1, TB, TB)
            add_x(1)
            ln_roots(2, TB, TB)
            ln_roots(3, 0, TB)
            add_ffn(0)
            add_ffn(2)
            for t in range(TB, NT):
                ln_roots(3, t, 1)
                if t % 2 == 0:
                    add_ffn(t)

        @block.scalar
        def _(act):
            def split_wa(par, count):
                act.wait_ge(wa_loaded[par], count)
                act.activation(wa_hi[:, par], wa_stage[:, par], ACT.Copy).then_inc(wa_hi_ready, 1)

            def norm_x(b):
                act.wait_ge(nmr_ready, b + 1)
                for t in range(TB * b, TB * b + TB, 2):
                    act.activation(y[:, t, :], y[:, t, :], ACT.Identity, bias=nmr[:, 0, t:t + 1],
                                   scale=rstd[:, 0, t:t + 1]).then_inc(x_normed[0], 1)

            def high_x(b):
                for t in range(TB * b, TB * b + TB):
                    act.wait_ge(x_turned, t + 1)
                    act.activation(xh[:, :, t * P:(t + 1) * P],
                                   ps[:, t, :].rearrange("p (c n) -> p c n", c=C), ACT.Copy).then_inc(xh_ready, 1)

            norm_x(0)
            split_wa(0, 16)
            high_x(0)
            split_wa(1, 16)
            act.wait_ge(tab_loaded, 16)
            norm_x(1)

            def bias_columns(h, par):
                act.activation(q_k_bias[:, par, :], tab[:, 0:2, bass.ds(h, 1)].rearrange(
                    "p w a -> p (w a)"), ACT.Copy).then_inc(bias_ready, 1)

            def square(par, g, count):
                w, b = g % 2, g // 2
                act.wait_ge(qk_product, count)
                act.activation(squares[:, par, w, b * S:(b + 1) * S], ps[:, 4 * par + g, :],
                               ACT.Square, bias=q_k_bias[:, par, w:w + 1]).then_inc(sq_ready, 1)

            bias_columns(0, 0)
            bias_columns(1, 1)
            act.wait_ge(bias_ready, 2)
            for pos, (par, g) in enumerate(FIRST):
                square(par, g, pos + 1)
                if pos == 3:
                    high_x(1)
                if pos == 5:
                    split_wa(0, 32)

            def phase_a(i, last=False):
                for par in range(2):
                    h = 2 * i + par
                    if not (last and par == 1):
                        split_wa(1 - par, 16 * (i + 1 + par))
                    bias_columns(h, par)
                    act.wait_ge(bias_ready, h + 1)
                    act.wait_ge(acc_ready, 2 * h + 2)
                    for g in range(4):
                        square(par, g, 4 * h + g + 1)

            def split_wv(pair, slot, c):
                act.activation(wv_hi[:, slot, c:c + 2, :], wv_stage[:, c:c + 2, :],
                               ACT.Copy).then_inc(wv_hi_ready, 1)

            def split_wo(pair, slot, h):
                act.activation(wo_hi[:, slot, h, :], wo_stage[:, h, :], ACT.Copy).then_inc(wo_hi_ready, 1)

            with act.Fori(1, PAIRS - 1) as i:
                phase_a(i)
            act.wait_ge(wv_loaded, 16)
            split_wv(0, 0, 0)
            split_wv(0, 0, 2)
            phase_a(PAIRS - 1, last=True)

            def evacuate_v(item, tile, bank):
                act.wait_ge(v_product, item)
                act.activation(vh[:, tile:tile + 2, :], ps[:, bank, :].rearrange("p (t n) -> p t n", t=2),
                               ACT.Copy).then_inc(vh_ready, 1)

            def prepare_qk(s, m):
                act.wait_ge(qk_scaled, m + 1)
                act.activation(qk_hi[:, s % 2], qk_in[:, s], ACT.Copy).then_inc(qk_hi_ready, 1)

            evacuate_v(1, 0, 0)
            evacuate_v(2, 2, 1)

            def spread(b):
                for w in range(2):
                    act.wait_ge(rms_spread, 2 * b + w + 1)
                    act.activation(rms_row[:, w, b * S:(b + 1) * S], ps[:, 4 + 2 * b + w, :],
                                   ACT.Copy).then_inc(rms_row_ready, 1)

            spread(0)
            prepare_qk(0, 0)
            evacuate_v(3, 4, 3)
            spread(1)
            evacuate_v(4, 6, 0)
            prepare_qk(1, 1)

            def evacuate_o(s, n, bank=WORK + 1):
                act.wait_ge(o_product, n + 1)
                sl, b = s % 2, s // 2
                act.activation(oth[:, sl, b * S:(b + 1) * S], ps[:, bank, :], ACT.Identity,
                               bias=v_bias[:, sl, :]).then_inc(oth_ready, 1)

            def exponentials(n, sl, i):
                act.wait_ge(max_ready, 4 * n + i + 1)
                act.activation(prob[:, i, :], ps[:, SCORE + i, :], ACT.Exp, bias=neg_max[:, sl, i:i + 1],
                               accum_out=row_sum[:, sl, i:i + 1]).then_inc(exp_ready, 1)

            def high_pt(n, i):
                act.wait_ge(pt_product, 4 * n + i + 1)
                act.activation(pth[:, :, i * P:(i + 1) * P],
                               ps[:, TRANS + i % 2, :].rearrange("p (k q) -> p k q", k=TB),
                               ACT.Copy).then_inc(pth_ready, 1)

            def v_bias_column(h, sl, n):
                act.activation(v_bias[:, sl, :], tab[:, 4, bass.ds(h, 1)], ACT.Copy).then_inc(bias_ready, 1)
                act.wait_ge(bias_ready, HEADS + n + 1)

            def step(p, s, weights, do_v=True, first=False):
                n = 4 * p + s
                h, b, sl = 2 * p + s % 2, s // 2, s % 2
                if not first:
                    evacuate_o((s - 1) % 4, n - 1)
                for i in range(TB):
                    exponentials(n, sl, i)
                for i in range(TB):
                    high_pt(n, i)
                    if i == 1 and do_v:
                        evacuate_v(n + 3, TB * (1 - b) + 2 * sl, WORK)
                prepare_qk((s + 2) % 4, n + 2)
                weights()
                v_bias_column(h, sl, n)

            def wo_pair(pair, slot):
                def both():
                    act.wait_ge(wo_loaded, 16 * pair + 16)
                    split_wo(pair, slot, 0)
                    split_wo(pair, slot, 1)
                return both

            def wv_pair(pair, slot):
                def both():
                    act.wait_ge(wv_loaded, 16 * pair + 16)
                    split_wv(pair, slot, 0)
                    split_wv(pair, slot, 2)
                return both

            def wo_part(pair, slot, h):
                def one():
                    act.wait_ge(wo_loaded, 16 * pair + 16)
                    split_wo(pair, slot, h)
                return one

            def wv_part(pair, slot, c):
                def one():
                    act.wait_ge(wv_loaded, 16 * pair + 16)
                    split_wv(pair, slot, c)
                return one

            def nothing():
                pass

            step(0, 0, wo_pair(0, 0), do_v=False, first=True)
            step(0, 1, wv_pair(1, 1), do_v=False)

            def pair_steps(p, par, last=False):
                step(p, 2, wo_part(p + 1, 1 - par, 0))
                step(p, 3, wo_part(p + 1, 1 - par, 1))
                step(p + 1, 0, nothing if last else wv_part(p + 2, par, 0))
                step(p + 1, 1, nothing if last else wv_part(p + 2, par, 2))

            with act.Fori(0, (PAIRS - 2) // 2) as i:
                pair_steps(2 * i, 0)
                pair_steps(2 * i + 1, 1)
            pair_steps(PAIRS - 2, 0, last=True)

            def ffn_weights():
                act.wait_ge(ffn_loaded, 16 * 4)
                act.activation(wb_hi, wb_stage[:, :, :], ACT.Copy).then_inc(ffn_hi_ready, 1)
                act.activation(in_hi[:, :], in_stage[:, :], ACT.Copy).then_inc(ffn_hi_ready, 1)
                act.activation(bt_hi, bt_stage[:, :], ACT.Copy).then_inc(ffn_hi_ready, 1)

            def norm_y(b):
                act.wait_ge(nmr_ready, 3 + 2 * b)
                for t in range(TB * b, TB * b + TB):
                    act.activation(y[:, t, :], y[:, t, :], ACT.Identity, bias=nmr[:, 1, t:t + 1],
                                   scale=rstd[:, 1, t:t + 1]).then_inc(y_normed, 1)

            def make_z(b):
                act.wait_ge(nmr_ready, 4 + 2 * b)
                for k in range(0, TB, 2):
                    t = TB * b + k
                    if b:
                        act.wait_ge(z_turned, k + 1)
                    act.activation(z[:, k, :], y[:, t, :], ACT.Identity, bias=nmr[:, 2, t:t + 1],
                                   scale=rstd[:, 2, t:t + 1]).then_inc(z_ready[0], 1)

            def high_z(b, tiles):
                for t in (TB * b + k for k in tiles):
                    act.wait_ge(z_turned, t + 1)
                    act.activation(xh[:, :, t * P:(t + 1) * P],
                                   ps[:, Z[b][t % TB], :].rearrange("p (c n) -> p c n", c=C),
                                   ACT.Copy).then_inc(zh_ready, 1)

            def gate_exps(b):
                gb = slice(TB * b, TB * b + TB)
                act.wait_ge(gate_in, 2 * b + 1)
                act.activation(g_e[:, gb, :], g_e[:, gb, :], ACT.Exp).then_inc(gate_exp, 1)
                act.wait_ge(gate_in, 2 * b + 2)
                act.activation(g_s[:, 1, gb], g_s[:, 0, gb], ACT.Exp, scale=-1.0).then_inc(gate_exp, 1)

            def high_hw(b):
                act.wait_ge(hw_turned, b + 1)
                act.activation(hw_hi[:, b, :], ps[:, HW[b], :], ACT.Copy).then_inc(hw_hi_ready, 1)

            def norm_ffn(t, count):
                act.wait_ge(nmr_ready, count)
                act.activation(x_again[:, t, :], x_again[:, t, :], ACT.Identity, bias=nmr[:, 3, t:t + 1],
                               scale=rstd[:, 3, t:t + 1]).then_inc(ffn_normed, 1)

            N = 4 * PAIRS - 2
            evacuate_o(1, N - 1)
            for i in range(TB):
                exponentials(N, 0, i)
            ffn_weights()
            v_bias_column(HEADS - 2, 0, N)
            v_bias_column(HEADS - 1, 1, N + 1)
            high_pt(N, 0)
            high_pt(N, 1)
            exponentials(N + 1, 1, 0)
            exponentials(N + 1, 1, 1)
            high_pt(N, 2)
            high_pt(N, 3)
            exponentials(N + 1, 1, 2)
            exponentials(N + 1, 1, 3)
            for i in range(TB):
                high_pt(N + 1, i)
                if i == 1:
                    evacuate_o(2, N)
            norm_y(0)
            evacuate_o(3, N + 1, bank=WORK)
            make_z(0)
            high_z(0, range(TB))
            norm_y(1)
            gate_exps(0)
            make_z(1)
            high_hw(0)
            high_z(1, range(TB))
            for t in range(TB):
                norm_ffn(t, 7)
            gate_exps(1)
            high_hw(1)
            for t in range(TB, NT):
                norm_ffn(t, t + 4)

        @block.tensor
        def _(pe):
            def three(outp, lhs, rhs, first, last):
                pe.matmul(outp, lhs[0], rhs[0], start=first, stop=False)
                pe.matmul(outp, lhs[0], rhs[1], start=False, stop=False)
                return pe.matmul(outp, lhs[1], rhs[0], start=False, stop=last)

            pe.wait_ge(const_ready, 4)

            def turn_x(b):
                for t in range(TB * b, TB * b + TB):
                    pe.wait_ge(x_normed[t % 2], t // 2 + 1)
                    for c in range(C):
                        ins = pe.transpose(ps[:, t, c * P:(c + 1) * P], y[:, t, c * P:(c + 1) * P], ident[:, :])
                    ins.then_inc(x_turned, 1)

            def q_or_k(par, g):
                w, b = g % 2, g // 2
                cols = slice(b * S, (b + 1) * S)
                for c in range(C):
                    ins = three(ps[:, 4 * par + g, :], (wa_hi[:, par, w, c], wa_lo[:, par, w, c]),
                                (xh[:, c, cols], xl[:, c, cols]), c == 0, c == C - 1)
                ins.then_inc(qk_product, 1)

            turn_x(0)
            pe.wait_ge(xl_ready, TB)
            for pos, (par, g) in enumerate(FIRST):
                if pos == 0 or pos == 2:
                    pe.wait_ge(wa_lo_ready, par + 1)
                if pos == 4:
                    pe.wait_ge(qk_out_ready, 4)
                    turn_x(1)
                    pe.wait_ge(xl_ready, NT)
                q_or_k(par, g)

            def phase_a(i):
                for par in range(2):
                    pe.wait_ge(wa_lo_ready, 2 * i + par + 1)
                    for g in range(4):
                        q_or_k(par, g)

            with pe.Fori(1, PAIRS) as i:
                phase_a(i)

            def v_item(slot, tile, bank):
                for k in range(2):
                    cols = slice((tile + k) * P, (tile + k + 1) * P)
                    for c in range(C):
                        ins = three(ps[:, bank, 2 * P * k:2 * P * (k + 1)], (xh[:, c, cols], xl[:, c, cols]),
                                    (wv_hi[:, slot, c], wv_lo[:, slot, c]), c == 0, c == C - 1)
                ins.then_inc(v_product, 1)

            pe.wait_ge(qk_out_ready, 4 * HEADS - 4)
            pe.wait_ge(wv_lo_ready, 2)
            v_item(0, 0, 0)
            v_item(0, 2, 1)
            pe.wait_ge(acc_ready, 4 + 2 * HEADS)
            for b in range(2):
                for w in range(2):
                    for t in range(TB):
                        col = NT * b + TB * w + t
                        tok = slice((TB * b + t) * P, (TB * b + t + 1) * P)
                        ins = pe.matmul(ps[:, 2 + 3 * b, col:col + 1], acc[:, w, tok], ones[:, 0:1],
                                        start=True, stop=True)
                ins.then_inc(col_sums, 1)
                if b == 0:
                    pe.wait_ge(qk_out_ready, 4 * HEADS)

            def spread(b):
                for w in range(2):
                    pe.wait_ge(diag_ready, 2 * b + w + 1)
                    pe.matmul(ps[:, 4 + 2 * b + w, :], ones[:, :], diag[:, 2 * b + w, :],
                              start=True, stop=True).then_inc(rms_spread, 1)

            v_item(0, 4, 3)
            spread(0)
            pe.wait_ge(vl_ready, 1)
            v_item(0, 6, 0)
            spread(1)
            pe.wait_ge(vl_ready, 4)

            def y_item(slot, tile, bank):
                cols = slice(tile * P, (tile + 1) * P)
                for h in range(2):
                    ins = three(ps[:, bank, :], (oth[:, h, cols], otl[:, h, cols]),
                                (wo_hi[:, slot, h, :], wo_lo[:, slot, h, :]), h == 0, h == 1)
                ins.then_inc(y_product, 1)

            def scores(n, sl):
                for i in range(TB):
                    rows = slice(i * P, (i + 1) * P)
                    three(ps[:, SCORE + i, :], (qk_hi[:, sl, 0, rows], qk_lo[:, sl, 0, rows]),
                          (qk_hi[:, sl, 1, :], qk_lo[:, sl, 1, :]), True, True).then_inc(scores_ready, 1)

            def turn_probs(n, i):
                pe.wait_ge(prob_ready, 4 * n + i + 1)
                if i >= 2:
                    pe.wait_ge(ptl_ready, 4 * n + i - 1)
                for k in range(TB):
                    ins = pe.transpose(ps[:, TRANS + i % 2, k * P:(k + 1) * P],
                                       prob[:, i, k * P:(k + 1) * P], ident[:, :])
                ins.then_inc(pt_product, 1)

            def attend(n, sl, b, bank):
                d = slice(sl * P, (sl + 1) * P)
                for half in range(2):
                    pe.wait_ge(ptl_ready, 4 * n + 2 * half + 2)
                    cols = slice(half * 2 * P, (half + 1) * 2 * P)
                    for k in range(TB):
                        ins = three(ps[:, bank, cols], (vh[:, TB * b + k, d], vl[:, TB * b + k, d]),
                                    (pth[:, k, cols], ptl[:, k, cols]), k == 0, k == TB - 1)
                ins.then_inc(o_product, 1)

            def step(p, s, par, do_v=True, y_items=2, first=False):
                n = 4 * p + s
                sl, b = s % 2, s // 2
                pe.wait_ge(qk_lo_ready, n + 1)
                if not first:
                    pe.wait_ge(prob_ready, 4 * n)
                if y_items:
                    pe.wait_ge(y_added, 2 * n - 2)
                scores(n, sl)
                if do_v:
                    pair = p + 1 if b else p
                    pe.wait_ge(wv_lo_ready, 2 * pair + 2)
                    pe.wait_ge(vl_ready, n + 2)
                    v_item(1 - par if b else par, TB * (1 - b) + 2 * sl, WORK)
                y_slot = par if b else 1 - par
                y_tile = (0 if b else TB) + 2 * sl
                for i in range(TB):
                    turn_probs(n, i)
                    if i == 1:
                        if not first:
                            pe.wait_ge(otl_ready, n)
                        if y_items:
                            pe.wait_ge(wo_lo_ready, 2 * (p if b else p - 1) + 2)
                            y_item(y_slot, y_tile, SCORE)
                if y_items:
                    y_item(y_slot, y_tile + 1, SCORE + 1)
                if not first:
                    pe.wait_ge(vl_ready, n + 2 - sl)
                attend(n, sl, b, WORK + 1)

            step(0, 0, 0, do_v=False, y_items=0, first=True)
            step(0, 1, 0, do_v=False, y_items=0)

            def pair_steps(p, par):
                step(p, 2, par)
                step(p, 3, par)
                step(p + 1, 0, 1 - par)
                step(p + 1, 1, 1 - par)

            with pe.Fori(0, (PAIRS - 2) // 2) as i:
                pair_steps(2 * i, 0)
                pair_steps(2 * i + 1, 1)
            pair_steps(PAIRS - 2, 0)

            N = 4 * PAIRS - 2
            pe.wait_ge(qk_lo_ready, N + 1)
            pe.wait_ge(prob_ready, 4 * N)
            pe.wait_ge(y_added, 2 * N - 2)
            scores(N, 0)
            pe.wait_ge(vl_ready, N + 2)
            pe.wait_ge(otl_ready, N)
            pe.wait_ge(wo_lo_ready, 2 * PAIRS)
            for t, bank in enumerate((WORK, WORK + 1, TRANS, TRANS + 1)):
                y_item(1, t, bank)
            for i in range(2):
                pe.wait_ge(y_added, 2 * N + 1 + i)
                turn_probs(N, i)
            pe.wait_ge(qk_lo_ready, N + 2)
            pe.wait_ge(prob_ready, 4 * N + 4)
            scores(N + 1, 1)
            turn_probs(N, 2)
            turn_probs(N, 3)
            attend(N, 0, 1, WORK + 1)
            for i in range(TB):
                turn_probs(N + 1, i)
            attend(N + 1, 1, 1, WORK)
            pe.wait_ge(otl_ready, N + 2)
            for i in range(TB):
                y_item(1, TB + i, SCORE + i)

            def turn_z(b, tiles):
                for k in tiles:
                    pe.wait_ge(z_ready[k % 2], 2 * b + k // 2 + 1)
                    for c in range(C):
                        ins = pe.transpose(ps[:, Z[b][k], c * P:(c + 1) * P],
                                           z[:, k, c * P:(c + 1) * P], ident[:, :])
                    ins.then_inc(z_turned, 1)

            def hidden(b):
                for k in range(TB):
                    t = TB * b + k
                    pe.wait_ge(zl_ready, t + 1)
                    cols = slice(t * P, (t + 1) * P)
                    half = slice(WIDE * (k % 2), WIDE * (k % 2 + 1))
                    for c in range(C):
                        rhs = slice(c * IN, c * IN + WIDE)
                        ins = three(ps[:, HIDDEN[b] + k // 2, half], (xh[:, c, cols], xl[:, c, cols]),
                                    (in_hi[:, rhs], in_lo[:, rhs]), c == 0, c == C - 1)
                ins.then_inc(hidden_ready, 1)

            def base(b, k):
                cols = slice((TB * b + k) * P, (TB * b + k + 1) * P)
                for c in range(C):
                    three(ps[:, BASE[b][k], :], (xh[:, c, cols], xl[:, c, cols]),
                          (wb_hi[:, c, :], wb_lo[:, c, :]), c == 0, False)

            def turn_hw(b):
                pe.wait_ge(hw_ready, b + 1)
                for k in range(TB):
                    ins = pe.transpose(ps[:, HW[b], k * P:(k + 1) * P], hw[:, b, k * P:(k + 1) * P], ident[:, :])
                ins.then_inc(hw_turned, 1)

            def experts(b, k):
                pe.wait_ge(hw_lo_ready, b + 1)
                cols = slice(k * P, (k + 1) * P)
                three(ps[:, BASE[b][k], :], (hw_hi[:, b, cols], hw_lo[:, b, cols]), (bt_hi, bt_lo),
                      False, True).then_inc(ffn_product, 1)

            turn_z(0, range(TB))
            pe.wait_ge(ffn_lo_ready, 3)
            pe.wait_ge(y_added, 2 * N + 2 + TB)
            hidden(0)
            for k in range(TB):
                base(0, k)
            turn_hw(0)
            turn_z(1, (0, 1, 2))
            for k in range(TB):
                experts(0, k)
            turn_z(1, (3,))
            pe.wait_ge(ffn_read, 2)
            hidden(1)
            pe.wait_ge(ffn_read, TB)
            for k in range(3):
                base(1, k)
            turn_hw(1)
            for k in range(3):
                experts(1, k)
            base(1, 3)
            experts(1, 3)

        @block.vector
        def _(dve):
            links, measured, roots = [0], [0], [0]

            def link(ins):
                links[0] += 1
                ins.then_inc(chain, 1)
                dve.wait_ge(chain, links[0])

            def tile_stats(src, stage, t):
                dve.bn_stats(stats[:, stage, t, :], src[:, t, :]).then_inc(stats_ready, 1)

            def tile_moments(stage, t):
                measured[0] += 1
                dve.wait_ge(stats_ready, measured[0])
                dve.bn_aggr(mv[:, stage, t, :], stats[:, stage, t, :]).then_inc(mv_ready, 1)

            def moments(src, stage, tiles, before=None):
                for j, t in enumerate(tiles):
                    if before:
                        before(t)
                    tile_stats(src, stage, t)
                    if j:
                        tile_moments(stage, tiles[j - 1])
                tile_moments(stage, tiles[-1])

            def variances(stage, t, k):
                tiles = slice(t, t + k)
                dve.wait_ge(mv_ready, measured[0])
                dve.tensor_scalar(var_eps[:, stage, tiles], mv[:, stage, tiles, 1], LN_EPS, None,
                                  ALU.add).then_inc(var_ready, 1)

            def wait_roots():
                roots[0] += 1
                dve.wait_ge(rstd_ready, roots[0])

            def offsets(stage, t, k):
                tiles = slice(t, t + k)
                wait_roots()
                dve.scalar_tensor_tensor(out=nmr[:, stage, tiles], in0=mv[:, stage, tiles, 0], scalar=-1.0,
                                         in1=rstd[:, stage, tiles], op0=ALU.mult,
                                         op1=ALU.mult).then_inc(nmr_ready, 1)

            def low_wa(par):
                dve.tensor_tensor(wa_lo[:, par], wa_stage[:, par], f32(wa_hi[:, par]),
                                  ALU.subtract).then_inc(wa_lo_ready, 1)

            def norm_x(b):
                moments(y, 0, range(TB * b, TB * b + TB), before=lambda t: dve.wait_ge(x_loaded[t], 16))
                variances(0, TB * b, TB)
                offsets(0, TB * b, TB)
                for t in range(TB * b + 1, TB * b + TB, 2):
                    dve.tensor_scalar(y[:, t, :], y[:, t, :], mv[:, 0, t, 0:1], rstd[:, 0, t:t + 1],
                                      ALU.subtract, ALU.mult).then_inc(x_normed[1], 1)

            def low_x(b):
                for t in range(TB * b, TB * b + TB):
                    dve.wait_ge(xh_ready, t + 1)
                    cols = slice(t * P, (t + 1) * P)
                    dve.tensor_tensor(xl[:, :, cols], ps[:, t, :].rearrange("p (c n) -> p c n", c=C),
                                      f32(xh[:, :, cols]), ALU.subtract).then_inc(xl_ready, 1)

            norm_x(0)
            dve.wait_ge(wa_hi_ready, 1)
            low_wa(0)
            low_x(0)
            dve.wait_ge(wa_hi_ready, 2)
            low_wa(1)
            norm_x(1)
            dve.wait_ge(tab_loaded, 16)

            def store_qk(par, g, h, count):
                w, b = g % 2, g // 2
                dve.wait_ge(sq_ready, count)
                dve.tensor_scalar(qk_out[:, par, w, b * S:(b + 1) * S], ps[:, 4 * par + g, :],
                                  tab[:, w, bass.ds(h, 1)], tab[:, 2 + w, bass.ds(h, 1)],
                                  ALU.add, ALU.mult).then_inc(qk_out_ready, 1)

            for pos, (par, g) in enumerate(FIRST):
                store_qk(par, g, par, pos + 1)
                if pos == 3:
                    low_x(1)
                if pos == 5:
                    dve.wait_ge(wa_hi_ready, 3)
                    low_wa(0)

            def phase_a(i, last=False):
                for par in range(2):
                    h = 2 * i + par
                    if not (last and par == 1):
                        dve.wait_ge(wa_hi_ready, h + 2)
                        low_wa(1 - par)
                    dve.wait_ge(stored[par], 16 * i)
                    for g in range(4):
                        store_qk(par, g, h, 4 * h + g + 1)

            with dve.Fori(1, PAIRS - 1) as i:
                phase_a(i)
            phase_a(PAIRS - 1, last=True)

            def split_v(item, tile, bank):
                dve.wait_ge(vh_ready, item)
                dve.tensor_tensor(vl[:, tile:tile + 2, :], ps[:, bank, :].rearrange("p (t n) -> p t n", t=2),
                                  f32(vh[:, tile:tile + 2, :]), ALU.subtract).then_inc(vl_ready, 1)

            split_v(1, 0, 0)
            split_v(2, 2, 1)
            for b in range(2):
                cols = slice(NT * b, NT * b + NT)
                dve.wait_ge(col_sums, b + 1)
                dve.tensor_scalar(sq_eps[:, cols], ps[:, 2 + 3 * b, cols], 1.0 / INNER, RMS_EPS,
                                  ALU.mult, ALU.add).then_inc(var_ready, 1)
            for b in range(2):
                dve.wait_ge(rms_ready, b + 1)
                for w in range(2):
                    for k in range(TB):
                        col = NT * b + TB * w + k
                        ins = dve.tensor_scalar(diag[:, 2 * b + w, k * P:(k + 1) * P], ident[:, :],
                                                rms[:, col:col + 1], 1.0 if w else SCORE_SCALE,
                                                ALU.mult, ALU.mult)
                    ins.then_inc(diag_ready, 1)
            split_v(3, 4, 3)
            split_v(4, 6, 0)
            dve.wait_ge(y_set, 16 * NT)
            dve.sem_inc(y_added, 2)

            def add_y(count, tile, bank):
                dve.wait_ge(y_product, count)
                return dve.tensor_tensor(y[:, tile, :], y[:, tile, :], ps[:, bank, :], ALU.add)

            def evacuate_o(h, s, n, bank=WORK + 1):
                sl, b = s % 2, s // 2
                cols = slice(b * S, (b + 1) * S)
                dve.wait_ge(oth_ready, n + 1)
                dve.scalar_tensor_tensor(out=otl[:, sl, cols], in0=ps[:, bank, :],
                                         scalar=tab[:, 4, bass.ds(h, 1)], in1=f32(oth[:, sl, cols]),
                                         op0=ALU.add, op1=ALU.subtract).then_inc(otl_ready, 1)

            def maximum(n, sl, i):
                dve.wait_ge(scores_ready, 4 * n + i + 1)
                dve.tensor_reduce(neg_max[:, sl, i:i + 1], ps[:, SCORE + i, :], AX.X, ALU.max,
                                  negate=True).then_inc(max_ready, 1)

            def normalize(n, sl, i):
                dve.wait_ge(exp_ready, 4 * n + i + 1)
                dve.reciprocal(row_inv[:, sl, i:i + 1], row_sum[:, sl, i:i + 1]).then_inc(inv_ready, 1)
                dve.wait_ge(inv_ready, 4 * n + i + 1)
                dve.tensor_scalar(prob[:, i, :], prob[:, i, :], row_inv[:, sl, i:i + 1], None,
                                  ALU.mult).then_inc(prob_ready, 1)

            def low_pt(n, i):
                dve.wait_ge(pth_ready, 4 * n + i + 1)
                rows = slice(i * P, (i + 1) * P)
                dve.tensor_tensor(ptl[:, :, rows], ps[:, TRANS + i % 2, :].rearrange("p (k q) -> p k q", k=TB),
                                  f32(pth[:, :, rows]), ALU.subtract).then_inc(ptl_ready, 1)

            def step(p, s, do_v=True, y_items=2, first=False):
                n = 4 * p + s
                b, sl = s // 2, s % 2
                for i in range(TB):
                    maximum(n, sl, i)
                    if i == 1 and not first:
                        evacuate_o(2 * p + 1 - sl if s else 2 * p - 1, (s - 1) % 4, n - 1)
                for i in range(TB):
                    normalize(n, sl, i)
                for i in range(TB):
                    low_pt(n, i)
                    if i == 1 and do_v:
                        split_v(n + 3, TB * (1 - b) + 2 * sl, WORK)
                for k in range(y_items):
                    add_y(2 * n - 3 + k, (0 if b else TB) + 2 * sl + k, SCORE + k).then_inc(y_added, 1)

            step(0, 0, do_v=False, y_items=0, first=True)
            step(0, 1, do_v=False, y_items=0)

            def pair_steps(p):
                step(p, 2)
                step(p, 3)
                step(p + 1, 0)
                step(p + 1, 1)

            with dve.Fori(0, (PAIRS - 2) // 2) as i:
                pair_steps(2 * i)
                pair_steps(2 * i + 1)
            pair_steps(PAIRS - 2)

            def add_x(t):
                if t % 2:
                    dve.wait_ge(y_normed, t + 1)
                    link(dve.tensor_tensor(y[:, t, :], y[:, t, :], x_again[:, t, :], ALU.add))
                else:
                    dve.wait_ge(x_added, t // 2 + 1)

            def make_z(b):
                for k in range(1, TB, 2):
                    t = TB * b + k
                    if b:
                        dve.wait_ge(z_turned, k + 1)
                    dve.tensor_scalar(z[:, k, :], y[:, t, :], mv[:, 2, t, 0:1], rstd[:, 2, t:t + 1],
                                      ALU.subtract, ALU.mult).then_inc(z_ready[1], 1)

            def low_z(k, b):
                t = TB * b + k
                dve.wait_ge(zh_ready, t + 1)
                cols = slice(t * P, (t + 1) * P)
                dve.tensor_tensor(xl[:, :, cols], ps[:, Z[b][k], :].rearrange("p (c n) -> p c n", c=C),
                                  f32(xh[:, :, cols]), ALU.subtract).then_inc(zl_ready, 1)

            def both(b):
                return ps[:, HIDDEN[b]:HIDDEN[b] + 2, :].rearrange("p j (i n) -> p (j i) n", n=WIDE)

            def over_experts(b, k):
                return g_s[:, k, TB * b:TB * b + TB].unsqueeze(2).broadcast_to([P, TB, E])

            def gate_arguments(b):
                gb = slice(TB * b, TB * b + TB)
                dve.wait_ge(hidden_ready, b + 1)
                link(dve.tensor_reduce(g_s[:, 2, gb], both(b)[:, :, P:P + E], AX.X, ALU.max))
                dve.tensor_tensor(g_e[:, gb, :], both(b)[:, :, P:P + E], over_experts(b, 2),
                                  ALU.subtract).then_inc(gate_in, 1)
                dve.tensor_scalar(g_s[:, 0, gb], both(b)[:, :, P + E], thr_bias[:, 0:1], None,
                                  ALU.add).then_inc(gate_in, 1)

            def gates(b):
                gb = slice(TB * b, TB * b + TB)
                dve.wait_ge(gate_exp, 2 * b + 2)
                dve.tensor_scalar(g_s[:, 5, gb], g_s[:, 1, gb], 8.0, 8.0, ALU.mult, ALU.add)
                link(dve.tensor_reduce(g_s[:, 3, gb], g_e[:, gb, :], AX.X, ALU.add))
                dve.reciprocal(g_s[:, 6, gb], g_s[:, 5, gb])
                link(dve.reciprocal(g_s[:, 4, gb], g_s[:, 3, gb]))
                link(dve.tensor_tensor(g_p[:, gb, :], g_e[:, gb, :], over_experts(b, 4), ALU.mult))
                link(dve.tensor_tensor(g_w[:, gb, :], g_p[:, gb, :], over_experts(b, 6), ALU.subtract))
                link(dve.tensor_scalar(g_p[:, gb, :], g_w[:, gb, :], 0.0, 2.0, ALU.max, ALU.mult))
                link(dve.tensor_reduce(g_s[:, 7, gb], g_p[:, gb, :], AX.X, ALU.add))
                link(dve.tensor_scalar(g_s[:, 8, gb], g_s[:, 7, gb], 0.0, None, ALU.is_equal))
                link(dve.scalar_tensor_tensor(out=g_s[:, 9, gb], in0=g_s[:, 7, gb], scalar=0.5,
                                              in1=g_s[:, 8, gb], op0=ALU.mult, op1=ALU.add))
                link(dve.reciprocal(g_s[:, 7, gb], g_s[:, 9, gb]))
                link(dve.tensor_tensor(g_w[:, gb, :], g_p[:, gb, :], over_experts(b, 7), ALU.mult))
                dve.tensor_tensor(hw[:, b, :].rearrange("p (t e r) -> p t e r", e=E, r=R),
                                  both(b)[:, :, 0:P].rearrange("p t (e r) -> p t e r", r=R),
                                  g_w[:, gb, :].unsqueeze(3).broadcast_to([P, TB, E, R]),
                                  ALU.mult).then_inc(hw_ready, 1)

            def low_hw(b):
                dve.wait_ge(hw_hi_ready, b + 1)
                dve.tensor_tensor(hw_lo[:, b, :], ps[:, HW[b], :], f32(hw_hi[:, b, :]),
                                  ALU.subtract).then_inc(hw_lo_ready, 1)

            def add_bias(t):
                dve.wait_ge(ffn_product, t + 1)
                return dve.tensor_tensor(x_again[:, t, :], ps[:, BASE[t // TB][t % TB], :], bb, ALU.add)

            def add_ffn(t):
                dve.wait_ge(ffn_normed, t + 1)
                dve.tensor_tensor(y[:, t, :], y[:, t, :], x_again[:, t, :], ALU.add).then_inc(out_ready[1], 1)

            N = 4 * PAIRS - 2
            added = 2 * N - 4
            maximum(N, 0, 0)
            maximum(N, 0, 1)
            evacuate_o(HEADS - 1, 1, N - 1)
            maximum(N, 0, 2)
            maximum(N, 0, 3)
            normalize(N, 0, 0)
            normalize(N, 0, 1)
            last_y = ((0, WORK), (1, WORK + 1), (2, TRANS), (3, TRANS + 1))
            for tile, bank in last_y[0:2]:
                add_y(added + tile + 1, tile, bank).then_inc(y_added, 1)
            normalize(N, 0, 2)
            normalize(N, 0, 3)
            for tile, bank in last_y[2:4]:
                add_y(added + tile + 1, tile, bank).then_inc(y_added, 1)
            dve.wait_ge(y_added, 2 * N + 2)
            tile_stats(y, 1, 0)
            low_pt(N, 0)
            low_pt(N, 1)
            for i in range(TB):
                maximum(N + 1, 1, i)
            low_pt(N, 2)
            low_pt(N, 3)
            for i in range(TB):
                normalize(N + 1, 1, i)
                if i % 2:
                    tile_stats(y, 1, 1 + i // 2)
            low_pt(N + 1, 0)
            low_pt(N + 1, 1)
            tile_stats(y, 1, 3)
            for t in range(TB):
                tile_moments(1, t)
            variances(1, 0, TB)
            evacuate_o(HEADS - 2, 2, N)
            low_pt(N + 1, 2)
            low_pt(N + 1, 3)
            offsets(1, 0, TB)
            evacuate_o(HEADS - 1, 3, N + 1, bank=WORK)

            moments(y, 2, range(TB), before=add_x)
            variances(2, 0, TB)
            for t in range(TB, TB + 2):
                add_y(added + t + 1, t, SCORE + t - TB).then_inc(y_added, 1)
            offsets(2, 0, TB)
            make_z(0)
            for t in range(TB + 2, NT):
                add_y(added + t + 1, t, SCORE + t - TB).then_inc(y_added, 1)
            dve.wait_ge(y_added, 2 * N + 2 + TB)
            moments(y, 1, range(TB, NT), before=lambda t: low_z(t - TB, 0))
            variances(1, TB, TB)
            offsets(1, TB, TB)
            gate_arguments(0)
            moments(y, 2, range(TB, NT), before=add_x)
            variances(2, TB, TB)
            gates(0)
            offsets(2, TB, TB)
            make_z(1)
            low_hw(0)
            for k in range(3):
                low_z(k, 1)
            dve.wait_ge(bb_loaded, 16)
            for t in range(TB):
                add_bias(t).then_inc(ffn_read, 1)
            low_z(3, 1)
            dve.wait_ge(ffn_read, TB)
            moments(x_again, 3, range(TB))
            variances(3, 0, TB)
            offsets(3, 0, TB)
            gate_arguments(1)
            gates(1)
            low_hw(1)
            add_ffn(1)
            add_ffn(3)
            for t in range(TB, NT):
                link(add_bias(t))
                moments(x_again, 3, (t,))
                variances(3, t, 1)
                offsets(3, t, 1)
                if t % 2:
                    add_ffn(t)


def kernel(L0_attn_hidden_states, L0_attn_Wq, L0_attn_bq, L0_attn_Wk, L0_attn_bk, L0_attn_Wv, L0_attn_bv,
           L0_attn_Wo, L0_attn_bo, L0_attn_gq, L0_attn_gk, L0_ffn_W_base, L0_ffn_b_base, L0_ffn_W_gate,
           L0_ffn_W_thr, L0_ffn_b_thr, L0_ffn_A, L0_ffn_B):
    import numpy as np
    import concourse.bacc as bacc
    from concourse.bass_utils import run_bass_kernel_spmd

    x = np.asarray(L0_attn_hidden_states)
    D, C = x.shape[-1], x.shape[-1] // P
    inner = L0_attn_Wq.shape[1]
    heads = inner // P

    def by_head(w, n):
        return np.asarray(w).reshape(C, P, inner // n, n).transpose(2, 1, 0, 3)

    def chunks(w):
        return np.asarray(w).reshape(C, P, -1).transpose(1, 0, 2)

    def columns(v):
        return np.asarray(v).reshape(heads, P).T

    def on_all(v):
        return np.broadcast_to(np.asarray(v), (P, v.shape[0]))

    gate = np.concatenate([np.asarray(L0_ffn_W_gate), np.asarray(L0_ffn_W_thr)])
    a_gate = chunks(np.concatenate([np.asarray(L0_ffn_A).reshape(-1, D), gate]).T)
    pad = 2 * P - a_gate.shape[2]
    a_gate = np.concatenate([a_gate.reshape(P, -1), np.zeros((P, pad), a_gate.dtype)], axis=1)
    arrays = {
        "x": x.reshape(-1, P, D),
        "w_qk": np.stack([by_head(L0_attn_Wq, P), by_head(L0_attn_Wk, P)], axis=2),
        "w_v": by_head(L0_attn_Wv, 2 * P),
        "w_o": np.asarray(L0_attn_Wo).reshape(heads // 2, 2, P, D).transpose(0, 2, 1, 3),
        "tables": np.stack([columns(v) for v in (L0_attn_bq, L0_attn_bk, L0_attn_gq, L0_attn_gk, L0_attn_bv)],
                           axis=1),
        "bo": on_all(L0_attn_bo),
        "w_base": chunks(np.asarray(L0_ffn_W_base).T),
        "w_in": a_gate,
        "b_t": np.asarray(L0_ffn_B).transpose(0, 2, 1).reshape(P, -1),
        "b_base": on_all(L0_ffn_b_base),
        "b_thr": on_all(L0_ffn_b_thr),
    }
    nc = bacc.Bacc("TRN2", target_bir_lowering=False, num_devices=1)
    arrays = {name: np.ascontiguousarray(a) for name, a in arrays.items()}
    aps = [nc.dram_tensor(name, a.shape, mybir.dt.from_np(a.dtype), kind="ExternalInput").ap()
           for name, a in arrays.items()]
    out = nc.dram_tensor("out", arrays["x"].shape, F32, kind="ExternalOutput").ap()
    build(nc, *aps, out)
    r = run_bass_kernel_spmd(nc, [arrays], core_ids=[0])
    return r.results[0]["out"].reshape(x.shape)
```

```python
from contextlib import ExitStack

import concourse.bass as bass
from concourse import mybir

F32 = mybir.dt.float32
F32R = mybir.dt.float32r
ALU = mybir.AluOpType
ACT = mybir.ActivationFunctionType
AX = mybir.AxisListType

P = 128


def build(nc, x, w_qk, w_v, w_o, tables, bo, w_base, w_in, b_t, b_base, b_thr, out):
    NT = x.shape[0]
    D = x.shape[2]
    C = D // P
    HEADS = w_qk.shape[0]
    INNER = HEADS * P
    PAIRS = HEADS // 2
    TB = NT // 2
    S = TB * P
    TOK = NT * P
    E = 8
    R = P // E
    IN = P + E + 1
    WIDE = 2 * P
    LN_EPS, RMS_EPS = 1e-5, 1e-6
    SCORE_SCALE = float(P) ** -0.5
    assert C == TB == 4 and S == 512

    BY_BATCH = [(par, g) for b in range(2) for par in range(2) for g in (2 * b, 2 * b + 1)]

    q_k_scratch = nc.dram_tensor("q_k_scratch", [HEADS, P, 2, TOK], F32, kind="Internal").ap()

    with ExitStack() as ctx:
        def sb(name, shape, dt=F32, stack=ctx):
            return stack.enter_context(nc.sbuf_tensor(name, shape, dt))

        def sem(name):
            return ctx.enter_context(nc.semaphore(name))

        ps = ctx.enter_context(nc.psum_tensor("ps", [P, 8, 512], F32))
        SCORE, TRANS, WORK = 0, 4, 6

        X = (0, 1, 2, 3, 2, 3, 6, 7)
        LAST_TRANS = (4, 5, 0, 1)

        Z = ((4, 5, 6, 7), (7, 2, 3, 6))
        HIDDEN = (2, 0)
        BASE = ((0, 1, 4, 5), (4, 5, 6, 7))
        HW = (6, 2)

        y = sb("y", [P, NT, D])
        xh = sb("xh", [P, C, TOK], F32R)
        xl = sb("xl", [P, C, TOK], F32R)
        ident = sb("ident", [P, P])
        ones = sb("ones", [P, P])
        tab = sb("tab", [P, 5, HEADS])
        wv_stage = sb("wv_stage", [P, C, 2 * P])
        wv_hi = sb("wv_hi", [P, 2, C, 2 * P], F32R)
        wv_lo = sb("wv_lo", [P, 2, C, 2 * P], F32R)
        wo_stage = sb("wo_stage", [P, 2, D])
        wb_stage = sb("wb_stage", [P, C, D])
        in_stage = sb("in_stage", [P, w_in.shape[1]])
        in_hi = sb("in_hi", [P, w_in.shape[1]], F32R)
        in_lo = sb("in_lo", [P, w_in.shape[1]], F32R)
        bt_stage = sb("bt_stage", [P, D])
        thr_bias = sb("thr_bias", [P, 1])
        stats = sb("stats", [P, 4, NT, 6])
        mv = sb("mv", [P, 4, NT, 2])
        var_eps = sb("var_eps", [P, 4, NT])
        rstd = sb("rstd", [P, 4, NT])
        nmr = sb("nmr", [P, 4, NT])
        sq_eps = sb("sq_eps", [P, 2 * NT])
        q_k_bias = sb("q_k_bias", [P, 2, 2])
        v_bias = sb("v_bias", [P, 2, 1])
        minus_half = sb("minus_half", [P, 2 * NT])
        rms = sb("rms", [P, 2 * NT])
        neg_max = sb("neg_max", [P, 2, TB])
        row_sum = sb("row_sum", [P, 2, TB])
        row_inv = sb("row_inv", [P, 2, TB])

        with ExitStack() as a_only:
            wa_stage = sb("wa_stage", [P, 2, 2, C, P], F32, a_only)
            wa_hi = sb("wa_hi", [P, 2, 2, C, P], F32R, a_only)
            wa_lo = sb("wa_lo", [P, 2, 2, C, P], F32R, a_only)
            qk_out = sb("qk_out", [P, 2, 2, TOK], F32, a_only)
            squares = sb("squares", [P, 2, 2, TOK], F32, a_only)
            acc = sb("acc", [P, 2, TOK], F32, a_only)

        vh = sb("vh", [P, NT, 2 * P], F32R)
        vl = sb("vl", [P, NT, 2 * P], F32R)
        oth = sb("oth", [P, 2, TOK], F32R)
        otl = sb("otl", [P, 2, TOK], F32R)
        pth = sb("pth", [P, TB, S], F32R)
        ptl = sb("ptl", [P, TB, S], F32R)
        wo_hi = sb("wo_hi", [P, 2, 2, D], F32R)
        wo_lo = sb("wo_lo", [P, 2, 2, D], F32R)
        qk_in = sb("qk_in", [P, 4, 2, S])
        qk_hi = sb("qk_hi", [P, 2, 2, S], F32R)
        qk_lo = sb("qk_lo", [P, 2, 2, S], F32R)
        rms_row = sb("rms_row", [P, 2, TOK])
        prob = sb("prob", [P, TB, S])

        def factors(b, w):
            return rms_row[:, w, b * S:(b + 1) * S]

        wb_hi = wv_hi[:, :, :, :].rearrange("p a c n -> p (a c n)").rearrange("p (c n) -> p c n", c=C)
        wb_lo = wv_lo[:, :, :, :].rearrange("p a c n -> p (a c n)").rearrange("p (c n) -> p c n", c=C)
        bt_hi, bt_lo = wo_hi[:, 0, 0, :], wo_lo[:, 0, 0, :]
        x_again = qk_in[:, :, :, :].rearrange("p a w n -> p (a w) n")
        z = prob
        hw = rms_row[:, 0, :].rearrange("p (b n) -> p b n", b=2)
        hw_hi, hw_lo = pth, ptl
        bb = wv_stage[:, 0:2, :].rearrange("p a n -> p (a n)")
        g_e = sb("g_e", [P, NT, E])
        g_p = sb("g_p", [P, NT, E])
        g_w = sb("g_w", [P, NT, E])
        g_s = sb("g_s", [P, 10, NT])

        x_loaded = [sem(f"x_loaded{t}") for t in range(NT)]
        tab_loaded = sem("tab_loaded")
        const_ready = sem("const_ready")
        stats_ready = sem("stats_ready")
        mv_ready = sem("mv_ready")
        chain = sem("chain")
        nmr_ready = sem("nmr_ready")
        var_ready = sem("var_ready")
        rstd_ready = sem("rstd_ready")
        x_normed = [sem("x_normed0"), sem("x_normed1")]
        x_turned = sem("x_turned")
        xh_ready = sem("xh_ready")
        xl_ready = sem("xl_ready")
        wa_loaded = [sem("wa_loaded0"), sem("wa_loaded1")]
        wa_hi_ready = sem("wa_hi_ready")
        wa_lo_ready = sem("wa_lo_ready")
        qk_product = sem("qk_product")
        bias_ready = sem("bias_ready")
        sq_ready = sem("sq_ready")
        qk_out_ready = sem("qk_out_ready")
        acc_ready = sem("acc_ready")
        stored = [sem("stored0"), sem("stored1")]
        col_sums = sem("col_sums")
        rms_ready = sem("rms_ready")
        diag_ready = sem("diag_ready")
        rms_spread = sem("rms_spread")
        rms_row_ready = sem("rms_row_ready")
        y_set = sem("y_set")
        wv_loaded = sem("wv_loaded")
        wo_loaded = sem("wo_loaded")
        wv_hi_ready = sem("wv_hi_ready")
        wv_lo_ready = sem("wv_lo_ready")
        wo_hi_ready = sem("wo_hi_ready")
        wo_lo_ready = sem("wo_lo_ready")
        qk_loaded = [sem(f"qk_loaded{s}") for s in range(4)]
        qk_scaled = sem("qk_scaled")
        qk_hi_ready = sem("qk_hi_ready")
        qk_lo_ready = sem("qk_lo_ready")
        scores_ready = sem("scores_ready")
        max_ready = sem("max_ready")
        exp_ready = sem("exp_ready")
        inv_ready = sem("inv_ready")
        prob_ready = sem("prob_ready")
        pt_product = sem("pt_product")
        pth_ready = sem("pth_ready")
        ptl_ready = sem("ptl_ready")
        v_product = sem("v_product")
        vh_ready = sem("vh_ready")
        vl_ready = sem("vl_ready")
        y_product = sem("y_product")
        o_product = sem("o_product")
        oth_ready = sem("oth_ready")
        otl_ready = sem("otl_ready")
        y_added = sem("y_added")
        ffn_loaded = sem("ffn_loaded")
        ffn_hi_ready = sem("ffn_hi_ready")
        ffn_lo_ready = sem("ffn_lo_ready")
        bb_loaded = sem("bb_loaded")
        x_reloaded = sem("x_reloaded")
        y_normed = sem("y_normed")
        x_added = sem("x_added")
        z_ready = [sem("z_ready0"), sem("z_ready1")]
        z_turned = sem("z_turned")
        zh_ready = sem("zh_ready")
        zl_ready = sem("zl_ready")
        hidden_ready = sem("hidden_ready")
        gate_in = sem("gate_in")
        gate_exp = sem("gate_exp")
        hw_ready = sem("hw_ready")
        hw_turned = sem("hw_turned")
        hw_hi_ready = sem("hw_hi_ready")
        hw_lo_ready = sem("hw_lo_ready")
        ffn_product = sem("ffn_product")
        ffn_read = sem("ffn_read")
        ffn_normed = sem("ffn_normed")
        out_ready = [sem("out_ready0"), sem("out_ready1")]
        out_stored = sem("out_stored")

        def f32(ap):
            return ap.bitcast(F32)

        block = ctx.enter_context(nc.Block())

        @block.sync
        def _(sp):
            def load_wa(h, par):
                return sp.dma_start(wa_stage[:, par], w_qk[bass.ds(h, 1)].rearrange(
                    "a p w c n -> p (a w) c n")).then_inc(wa_loaded[par], 16)

            for t in range(TB):
                sp.dma_start(y[:, t, :], x[t]).then_inc(x_loaded[t], 16)
            load_wa(0, 0)
            load_wa(1, 1)
            sp.dma_start(tab[:, :, :], tables).then_inc(tab_loaded, 16)
            for t in range(TB, NT):
                sp.dma_start(y[:, t, :], x[t]).then_inc(x_loaded[t], 16)
            sp.dma_start(wv_stage[:, :, :], w_v[0]).then_inc(wv_loaded, 16)
            sp.dma_start(wo_stage[:, :, :], w_o[0]).then_inc(wo_loaded, 16)
            sp.wait_ge(x_turned, NT)
            for t in range(NT):
                sp.dma_start(y[:, t, :], bo).then_inc(y_set, 16)

            def phase_a(i, by_batch=False, last=False):
                for par in range(2):
                    if not last:
                        sp.wait_ge(wa_lo_ready, 2 * i + par + 1)
                        load_wa(2 * i + 2 + par, par)
                    sp.wait_ge(qk_out_ready, 8 * i + (6 + 2 * par if by_batch else 4 * par + 4))
                    sp.dma_start(q_k_scratch[bass.ds(2 * i + par, 1)].rearrange("a p w n -> p (a w) n"),
                                 qk_out[:, par]).then_inc(stored[par], 16)

            phase_a(0, by_batch=True)
            with sp.Fori(1, PAIRS - 1) as i:
                phase_a(i)

            def load_qk(pair, s):
                src = q_k_scratch[bass.ds(2 * pair + s % 2, 1), :, :, (s // 2) * S:(s // 2 + 1) * S]
                sp.dma_start(qk_in[:, s], src.rearrange("a p w n -> p (a w) n")).then_inc(qk_loaded[s], 16)

            sp.wait_ge(stored[0], 16 * (PAIRS - 1))
            sp.wait_ge(stored[1], 16 * (PAIRS - 1))
            for s in range(4):
                load_qk(0, s)
            sp.wait_ge(wv_lo_ready, 2)
            sp.dma_start(wv_stage[:, :, :], w_v[1]).then_inc(wv_loaded, 16)
            phase_a(PAIRS - 1, by_batch=True, last=True)
            sp.wait_ge(stored[0], 16 * PAIRS)
            sp.wait_ge(stored[1], 16 * PAIRS)
            sp.dma_start(wb_stage[:, :, :], w_base).then_inc(ffn_loaded, 16)
            sp.dma_start(in_stage[:, :], w_in).then_inc(ffn_loaded, 16)
            sp.dma_start(bt_stage[:, :], b_t).then_inc(ffn_loaded, 16)
            sp.dma_start(thr_bias[:, :], b_thr).then_inc(ffn_loaded, 16)

            def phase_b(p, last=False):
                for s in range(4):
                    sp.wait_ge(qk_lo_ready, 4 * p + s + 1)
                    load_qk(p + 1, s)
                    if s == 0:
                        sp.wait_ge(wo_lo_ready, 2 * p + 2)
                        sp.dma_start(wo_stage[:, :, :], w_o[bass.ds(p + 1, 1)].rearrange(
                            "a p h n -> p (a h) n")).then_inc(wo_loaded, 16)
                    if s == 2 and not last:
                        sp.wait_ge(wv_lo_ready, 2 * p + 4)
                        sp.dma_start(wv_stage[:, :, :], w_v[bass.ds(p + 2, 1)].rearrange(
                            "a p c n -> p (a c) n")).then_inc(wv_loaded, 16)

            with sp.Fori(0, PAIRS - 2) as p:
                phase_b(p)
            phase_b(PAIRS - 2, last=True)

            sp.wait_ge(qk_lo_ready, 4 * PAIRS)
            for t in range(NT):
                sp.dma_start(x_again[:, t, :], x[t]).then_inc(x_reloaded, 16)
            sp.wait_ge(wv_lo_ready, 2 * PAIRS)
            sp.dma_start(bb, b_base).then_inc(bb_loaded, 16)
            for t in range(NT):
                sp.wait_ge(out_ready[t % 2], t // 2 + 1)
                sp.dma_start(out[t], y[:, t, :]).then_inc(out_stored, 16)
            sp.wait_ge(out_stored, 16 * NT)

        @block.gpsimd
        def _(pool):
            pool.memset(ident[:, :], 0.0).then_inc(const_ready, 1)
            pool.memset(ones[:, :], 1.0).then_inc(const_ready, 1)
            pool.memset(minus_half[:, :], -0.5).then_inc(const_ready, 1)
            pool.wait_ge(const_ready, 3)
            pool.affine_select(out=ident[:, :], in_=ident[:, :], compare_op=ALU.not_equal, fill=1.0,
                               base=0, pattern=[[-1, P]], channel_multiplier=1).then_inc(const_ready, 1)

            roots = [0]

            def inverse_root(dst, src, done):
                roots[0] += 1
                pool.wait_ge(var_ready, roots[0])
                pool.tensor_tensor(dst, src, minus_half[:, 0:src.shape[1]], ALU.pow).then_inc(done, 1)

            def ln_roots(stage, t, k):
                inverse_root(rstd[:, stage, t:t + k], var_eps[:, stage, t:t + k], rstd_ready)

            for w in range(2):
                pool.memset(acc[:, w, :], 0.0).then_inc(acc_ready, 2)
            for t in range(0, NT, 2):
                ln_roots(0, t, 2)

            def phase_a(i, first=False):
                for par in range(2):
                    h = 2 * i + par
                    pool.wait_ge(acc_ready, 2 * h + 4)
                    for w in range(2):
                        pool.wait_ge(sq_ready, 5 + 2 * par + w if first else 4 * h + 3 + w)
                        pool.tensor_tensor(acc[:, w, :], acc[:, w, :], squares[:, par, w, :],
                                           ALU.add).then_inc(acc_ready, 1)

            def split_weights(hi_ready, lo_ready, count, lo, stage, hi):
                pool.wait_ge(hi_ready, count)
                pool.tensor_tensor(lo, stage, f32(hi), ALU.subtract).then_inc(lo_ready, 1)

            def split_wv(pair, slot, c):
                split_weights(wv_hi_ready, wv_lo_ready, 2 * pair + c // 2 + 1,
                              wv_lo[:, slot, c:c + 2, :], wv_stage[:, c:c + 2, :], wv_hi[:, slot, c:c + 2, :])

            def split_wo(pair, slot, h):
                split_weights(wo_hi_ready, wo_lo_ready, 2 * pair + h + 1,
                              wo_lo[:, slot, h, :], wo_stage[:, h, :], wo_hi[:, slot, h, :])

            phase_a(0, first=True)
            with pool.Fori(1, PAIRS - 1) as i:
                phase_a(i)
            split_wv(0, 0, 0)
            split_wv(0, 0, 2)

            def add_squares(pos):
                par, g = BY_BATCH[pos]
                w, cols = g % 2, slice(g // 2 * S, (g // 2 + 1) * S)
                pool.wait_ge(acc_ready, 2 * HEADS if pos < 2 else 2 * HEADS + pos - 1)
                pool.wait_ge(sq_ready, 8 * (PAIRS - 1) + pos + 1)
                pool.tensor_tensor(acc[:, w, cols], acc[:, w, cols], squares[:, par, w, cols],
                                   ALU.add).then_inc(acc_ready, 1)

            def rms_roots(b):
                cols = slice(NT * b, NT * b + NT)
                inverse_root(rms[:, cols], sq_eps[:, cols], rms_ready)

            def scale_qk(p, s):
                b = s // 2
                pool.wait_ge(qk_loaded[s], 16 * p + 16)
                pool.tensor_tensor(qk_in[:, s], qk_in[:, s], rms_row[:, :, b * S:(b + 1) * S],
                                   ALU.mult).then_inc(qk_scaled, 1)

            def low_qk(s, m):
                pool.wait_ge(qk_hi_ready, m + 1)
                pool.tensor_tensor(qk_lo[:, s % 2], qk_in[:, s], f32(qk_hi[:, s % 2]),
                                   ALU.subtract).then_inc(qk_lo_ready, 1)

            def prepare_qk(p, s, m):
                scale_qk(p, s)
                low_qk(s, m)

            for pos in range(4):
                add_squares(pos)
            rms_roots(0)
            for pos in range(4, 7):
                add_squares(pos)
            pool.wait_ge(rms_row_ready, 2)
            scale_qk(0, 0)
            add_squares(7)
            low_qk(0, 0)
            rms_roots(1)
            prepare_qk(0, 1, 1)
            split_wv(1, 1, 0)
            split_wv(1, 1, 2)
            pool.wait_ge(rms_row_ready, 4)
            prepare_qk(0, 2, 2)
            split_wo(0, 0, 0)
            split_wo(0, 0, 1)
            prepare_qk(0, 3, 3)

            def pair_steps(p, par, last=False):
                for s in range(4):
                    prepare_qk(p + 1, s, 4 * p + 4 + s)
                    if s < 2:
                        split_wo(p + 1, 1 - par, s)
                    elif not last:
                        split_wv(p + 2, par, 2 * (s - 2))

            with pool.Fori(0, (PAIRS - 2) // 2) as i:
                pair_steps(2 * i, 0)
                pair_steps(2 * i + 1, 1)
            pair_steps(PAIRS - 2, 0, last=True)

            pool.wait_ge(ffn_hi_ready, 3)
            pool.tensor_tensor(wb_lo, wb_stage[:, :, :], f32(wb_hi), ALU.subtract).then_inc(ffn_lo_ready, 1)
            pool.tensor_tensor(in_lo[:, :], in_stage[:, :], f32(in_hi[:, :]), ALU.subtract).then_inc(ffn_lo_ready, 1)
            pool.tensor_tensor(bt_lo, bt_stage[:, :], f32(bt_hi), ALU.subtract).then_inc(ffn_lo_ready, 1)

            def add_x(b):
                for t in range(TB * b + 1, TB * b + TB, 2):
                    pool.wait_ge(y_normed, t - b)
                    pool.tensor_tensor(y[:, t, :], y[:, t, :], x_again[:, t, :], ALU.add).then_inc(x_added, 1)

            def add_ffn(t):
                pool.wait_ge(ffn_normed, t + 1)
                pool.tensor_tensor(y[:, t, :], y[:, t, :], x_again[:, t, :], ALU.add).then_inc(out_ready[0], 1)

            ln_roots(1, 0, TB)
            pool.wait_ge(x_reloaded, 16 * NT)
            add_x(0)
            ln_roots(2, 0, TB)
            ln_roots(1, TB, TB)
            add_x(1)
            ln_roots(2, TB, TB)
            ln_roots(3, 0, TB)
            add_ffn(0)
            add_ffn(2)
            for t in range(TB, NT):
                ln_roots(3, t, 1)
                if t == TB + 2:
                    add_ffn(TB)
            add_ffn(TB + 2)

        @block.scalar
        def _(act):
            def split_wa(par, count):
                act.wait_ge(wa_loaded[par], count)
                act.activation(wa_hi[:, par], wa_stage[:, par], ACT.Copy).then_inc(wa_hi_ready, 1)

            def norm_x(*tiles):
                for t in tiles:
                    act.wait_ge(nmr_ready, t // 2 + 1)
                    act.activation(y[:, t, :], y[:, t, :], ACT.Identity, bias=nmr[:, 0, t:t + 1],
                                   scale=rstd[:, 0, t:t + 1]).then_inc(x_normed[0], 1)

            def high_x(b):
                for t in range(TB * b, TB * b + TB):
                    act.wait_ge(x_turned, t + 1)
                    act.activation(xh[:, :, t * P:(t + 1) * P],
                                   ps[:, X[t], :].rearrange("p (c n) -> p c n", c=C), ACT.Copy).then_inc(xh_ready, 1)

            norm_x(0)
            split_wa(0, 16)
            norm_x(2)
            high_x(0)
            split_wa(1, 16)
            act.wait_ge(tab_loaded, 16)
            norm_x(4, 6)

            def bias_columns(h, par):
                act.activation(q_k_bias[:, par, :], tab[:, 0:2, bass.ds(h, 1)].rearrange(
                    "p w a -> p (w a)"), ACT.Copy).then_inc(bias_ready, 1)

            def square(par, g, count):
                w, b = g % 2, g // 2
                act.wait_ge(qk_product, count)
                act.activation(squares[:, par, w, b * S:(b + 1) * S], ps[:, 4 * par + g, :],
                               ACT.Square, bias=q_k_bias[:, par, w:w + 1]).then_inc(sq_ready, 1)

            bias_columns(0, 0)
            bias_columns(1, 1)
            act.wait_ge(bias_ready, 2)
            for pos, (par, g) in enumerate(BY_BATCH):
                square(par, g, pos + 1)
                if pos == 2:
                    high_x(1)
                if pos == 5:
                    split_wa(0, 32)

            def phase_a(i):
                for par in range(2):
                    split_wa(1 - par, 16 * (i + 1 + par))
                    bias_columns(2 * i + par, par)
                    act.wait_ge(bias_ready, 2 * i + par + 1)
                    act.wait_ge(acc_ready, 4 * i + 2 * par + 2)
                    for g in range(4):
                        square(par, g, 8 * i + 4 * par + g + 1)

            def split_wv(pair, slot, c):
                act.activation(wv_hi[:, slot, c:c + 2, :], wv_stage[:, c:c + 2, :],
                               ACT.Copy).then_inc(wv_hi_ready, 1)

            def split_wo(pair, slot, h):
                act.activation(wo_hi[:, slot, h, :], wo_stage[:, h, :], ACT.Copy).then_inc(wo_hi_ready, 1)

            with act.Fori(1, PAIRS - 1) as i:
                phase_a(i)
            act.wait_ge(wv_loaded, 16)
            split_wv(0, 0, 0)
            split_wv(0, 0, 2)
            split_wa(1, 16 * PAIRS)
            for pos, (par, g) in enumerate(BY_BATCH[0:7]):
                if pos == 0 or pos == 2:
                    act.wait_ge(acc_ready, 2 * HEADS - 2 + pos)
                    bias_columns(HEADS - 2 + par, par)
                    act.wait_ge(bias_ready, HEADS - 1 + par)
                square(par, g, 8 * (PAIRS - 1) + pos + 1)

            def evacuate_v(item, tile, bank):
                act.wait_ge(v_product, item)
                act.activation(vh[:, tile:tile + 2, :], ps[:, bank, :].rearrange("p (t n) -> p t n", t=2),
                               ACT.Copy).then_inc(vh_ready, 1)

            def prepare_qk(s, m):
                act.wait_ge(qk_scaled, m + 1)
                act.activation(qk_hi[:, s % 2], qk_in[:, s], ACT.Copy).then_inc(qk_hi_ready, 1)

            def spread(b, banks):
                for w in range(2):
                    act.wait_ge(rms_spread, 2 * b + w + 1)
                    act.activation(factors(b, w), ps[:, banks[w], :],
                                   ACT.Copy).then_inc(rms_row_ready, 1)

            spread(0, (4, 5))
            square(*BY_BATCH[7], 8 * PAIRS)
            prepare_qk(0, 0)
            evacuate_v(1, 0, 1)
            evacuate_v(2, 2, WORK + 1)
            act.wait_ge(wv_loaded, 32)
            split_wv(1, 1, 0)
            split_wv(1, 1, 2)
            prepare_qk(1, 1)
            act.wait_ge(stored[0], 16 * PAIRS)
            act.wait_ge(stored[1], 16 * PAIRS)

            def evacuate_o(s, n, bank=WORK + 1):
                act.wait_ge(o_product, n + 1)
                sl, b = s % 2, s // 2
                act.activation(oth[:, sl, b * S:(b + 1) * S], ps[:, bank, :], ACT.Identity,
                               bias=v_bias[:, sl, :]).then_inc(oth_ready, 1)

            def exponentials(n, sl, i):
                act.wait_ge(max_ready, 4 * n + i + 1)
                act.activation(prob[:, i, :], ps[:, SCORE + i, :], ACT.Exp, bias=neg_max[:, sl, i:i + 1],
                               accum_out=row_sum[:, sl, i:i + 1]).then_inc(exp_ready, 1)

            def high_pt(n, i, bank=None):
                act.wait_ge(pt_product, 4 * n + i + 1)
                act.activation(pth[:, :, i * P:(i + 1) * P],
                               ps[:, TRANS + i % 2 if bank is None else bank, :].rearrange("p (k q) -> p k q", k=TB),
                               ACT.Copy).then_inc(pth_ready, 1)

            def v_bias_column(h, sl, n):
                act.activation(v_bias[:, sl, :], tab[:, 4, bass.ds(h, 1)], ACT.Copy).then_inc(bias_ready, 1)
                act.wait_ge(bias_ready, HEADS + n + 1)

            def step(p, s, weights, first=False):
                n = 4 * p + s
                h, b, sl = 2 * p + s % 2, s // 2, s % 2
                if not first:
                    evacuate_o((s - 1) % 4, n - 1)
                for i in range(TB):
                    exponentials(n, sl, i)
                for i in range(TB):
                    high_pt(n, i)
                    if i == 1:
                        evacuate_v(n + 3, TB * (1 - b) + 2 * sl, WORK)
                        if first:
                            spread(1, (WORK + 1, SCORE))
                prepare_qk((s + 2) % 4, n + 2)
                weights()
                v_bias_column(h, sl, n)

            def wo_part(pair, slot, h):
                def one():
                    act.wait_ge(wo_loaded, 16 * pair + 16)
                    split_wo(pair, slot, h)
                return one

            def wv_part(pair, slot, c):
                def one():
                    act.wait_ge(wv_loaded, 16 * pair + 16)
                    split_wv(pair, slot, c)
                return one

            def nothing():
                pass

            def first_wo():
                act.wait_ge(wo_loaded, 16)
                split_wo(0, 0, 0)
                split_wo(0, 0, 1)

            step(0, 0, first_wo, first=True)
            step(0, 1, nothing)

            def pair_steps(p, par, last=False):
                step(p, 2, wo_part(p + 1, 1 - par, 0))
                step(p, 3, wo_part(p + 1, 1 - par, 1))
                step(p + 1, 0, nothing if last else wv_part(p + 2, par, 0))
                step(p + 1, 1, nothing if last else wv_part(p + 2, par, 2))

            with act.Fori(0, (PAIRS - 2) // 2) as i:
                pair_steps(2 * i, 0)
                pair_steps(2 * i + 1, 1)
            pair_steps(PAIRS - 2, 0, last=True)

            def ffn_weights():
                act.wait_ge(ffn_loaded, 16 * 4)
                act.activation(wb_hi, wb_stage[:, :, :], ACT.Copy).then_inc(ffn_hi_ready, 1)
                act.activation(in_hi[:, :], in_stage[:, :], ACT.Copy).then_inc(ffn_hi_ready, 1)
                act.activation(bt_hi, bt_stage[:, :], ACT.Copy).then_inc(ffn_hi_ready, 1)

            def norm_y(b):
                act.wait_ge(nmr_ready, 5 + 2 * b)
                for t in range(TB * b + 1, TB * b + TB):
                    act.activation(y[:, t, :], y[:, t, :], ACT.Identity, bias=nmr[:, 1, t:t + 1],
                                   scale=rstd[:, 1, t:t + 1]).then_inc(y_normed, 1)

            def make_z(b):
                act.wait_ge(nmr_ready, 6 + 2 * b)
                for k in range(0, TB, 2):
                    t = TB * b + k
                    if b:
                        act.wait_ge(z_turned, k + 1)
                    act.activation(z[:, k, :], y[:, t, :], ACT.Identity, bias=nmr[:, 2, t:t + 1],
                                   scale=rstd[:, 2, t:t + 1]).then_inc(z_ready[0], 1)

            def high_z(b, tiles):
                for t in (TB * b + k for k in tiles):
                    act.wait_ge(z_turned, t + 1)
                    act.activation(xh[:, :, t * P:(t + 1) * P],
                                   ps[:, Z[b][t % TB], :].rearrange("p (c n) -> p c n", c=C),
                                   ACT.Copy).then_inc(zh_ready, 1)

            def gate_exps(b):
                gb = slice(TB * b, TB * b + TB)
                act.wait_ge(gate_in, 2 * b + 1)
                act.activation(g_e[:, gb, :], g_e[:, gb, :], ACT.Exp).then_inc(gate_exp, 1)
                act.wait_ge(gate_in, 2 * b + 2)
                act.activation(g_s[:, 1, gb], g_s[:, 0, gb], ACT.Exp, scale=-1.0).then_inc(gate_exp, 1)

            def high_hw(b):
                act.wait_ge(hw_turned, b + 1)
                act.activation(hw_hi[:, b, :], ps[:, HW[b], :], ACT.Copy).then_inc(hw_hi_ready, 1)

            def norm_ffn(t, count):
                act.wait_ge(nmr_ready, count)
                act.activation(x_again[:, t, :], x_again[:, t, :], ACT.Identity, bias=nmr[:, 3, t:t + 1],
                               scale=rstd[:, 3, t:t + 1]).then_inc(ffn_normed, 1)

            N = 4 * PAIRS - 2
            evacuate_o(1, N - 1)
            for i in range(TB):
                exponentials(N, 0, i)
            ffn_weights()
            v_bias_column(HEADS - 2, 0, N)
            v_bias_column(HEADS - 1, 1, N + 1)
            high_pt(N, 0)
            high_pt(N, 1)
            exponentials(N + 1, 1, 0)
            exponentials(N + 1, 1, 1)
            high_pt(N, 2)
            high_pt(N, 3)
            exponentials(N + 1, 1, 2)
            exponentials(N + 1, 1, 3)
            for i in range(TB):
                high_pt(N + 1, i, LAST_TRANS[i])
            evacuate_o(2, N)
            evacuate_o(3, N + 1, bank=WORK)
            norm_y(0)
            make_z(0)
            high_z(0, range(TB))
            norm_y(1)
            gate_exps(0)
            make_z(1)
            high_hw(0)
            high_z(1, range(TB))
            for t in range(TB):
                norm_ffn(t, 9)
            gate_exps(1)
            high_hw(1)
            for t in range(TB, NT - 1):
                norm_ffn(t, t + 6)

        @block.tensor
        def _(pe):
            def three(outp, lhs, rhs, first, last):
                pe.matmul(outp, lhs[0], rhs[0], start=first, stop=False)
                pe.matmul(outp, lhs[0], rhs[1], start=False, stop=False)
                return pe.matmul(outp, lhs[1], rhs[0], start=False, stop=last)

            pe.wait_ge(const_ready, 4)

            def turn_x(b):
                for t in range(TB * b, TB * b + TB):
                    pe.wait_ge(x_normed[t % 2], t // 2 + 1)
                    for c in range(C):
                        ins = pe.transpose(ps[:, X[t], c * P:(c + 1) * P], y[:, t, c * P:(c + 1) * P], ident[:, :])
                    ins.then_inc(x_turned, 1)

            def q_or_k(par, g):
                w, b = g % 2, g // 2
                cols = slice(b * S, (b + 1) * S)
                for c in range(C):
                    ins = three(ps[:, 4 * par + g, :], (wa_hi[:, par, w, c], wa_lo[:, par, w, c]),
                                (xh[:, c, cols], xl[:, c, cols]), c == 0, c == C - 1)
                ins.then_inc(qk_product, 1)

            turn_x(0)
            pe.wait_ge(xl_ready, TB)
            for pos, (par, g) in enumerate(BY_BATCH):
                if pos == 0 or pos == 2:
                    pe.wait_ge(wa_lo_ready, par + 1)
                if pos == 3:
                    turn_x(1)
                if pos == 4:
                    pe.wait_ge(xl_ready, NT)
                q_or_k(par, g)

            def phase_a(i):
                for par in range(2):
                    pe.wait_ge(wa_lo_ready, 2 * i + par + 1)
                    for g in range(4):
                        q_or_k(par, g)

            with pe.Fori(1, PAIRS - 1) as i:
                phase_a(i)

            def v_item(slot, tile, bank):
                for k in range(2):
                    cols = slice((tile + k) * P, (tile + k + 1) * P)
                    for c in range(C):
                        ins = three(ps[:, bank, 2 * P * k:2 * P * (k + 1)], (xh[:, c, cols], xl[:, c, cols]),
                                    (wv_hi[:, slot, c], wv_lo[:, slot, c]), c == 0, c == C - 1)
                ins.then_inc(v_product, 1)

            def column_sums(b, bank):
                for w in range(2):
                    for t in range(TB):
                        col = NT * b + TB * w + t
                        tok = slice((TB * b + t) * P, (TB * b + t + 1) * P)
                        ins = pe.matmul(ps[:, bank, col:col + 1], acc[:, w, tok], ones[:, 0:1],
                                        start=True, stop=True)
                ins.then_inc(col_sums, 1)

            def spread(b, banks):
                for w in range(2):
                    pe.wait_ge(diag_ready, 2 * b + w + 1)
                    pe.matmul(ps[:, banks[w], :], ones[:, :], factors(b, w),
                              start=True, stop=True).then_inc(rms_spread, 1)

            done = 8 * (PAIRS - 1)
            for pos, (par, g) in enumerate(BY_BATCH):
                if pos == 0 or pos == 2:
                    pe.wait_ge(wa_lo_ready, HEADS - 1 + par)
                q_or_k(par, g)
                if pos == 4:
                    pe.wait_ge(acc_ready, 2 * HEADS + 4)
                    pe.wait_ge(qk_out_ready, done + 4)
                    column_sums(0, 0)
                if pos == 6:
                    spread(0, (4, 5))
            pe.wait_ge(wv_lo_ready, 2)
            v_item(0, 0, 1)
            pe.wait_ge(acc_ready, 2 * HEADS + 8)
            pe.wait_ge(qk_out_ready, done + 8)
            column_sums(1, 2)
            v_item(0, 2, WORK + 1)
            pe.wait_ge(var_ready, 6)
            pe.wait_ge(rms_row_ready, 2)
            pe.wait_ge(vl_ready, 1)

            def y_item(slot, tile, bank):
                cols = slice(tile * P, (tile + 1) * P)
                for h in range(2):
                    ins = three(ps[:, bank, :], (oth[:, h, cols], otl[:, h, cols]),
                                (wo_hi[:, slot, h, :], wo_lo[:, slot, h, :]), h == 0, h == 1)
                ins.then_inc(y_product, 1)

            def scores(n, sl):
                for i in range(TB):
                    rows = slice(i * P, (i + 1) * P)
                    three(ps[:, SCORE + i, :], (qk_hi[:, sl, 0, rows], qk_lo[:, sl, 0, rows]),
                          (qk_hi[:, sl, 1, :], qk_lo[:, sl, 1, :]), True, True).then_inc(scores_ready, 1)

            def turn_probs(n, i, bank=None):
                pe.wait_ge(prob_ready, 4 * n + i + 1)
                if bank is None:
                    bank = TRANS + i % 2
                    if i >= 2:
                        pe.wait_ge(ptl_ready, 4 * n + i - 1)
                for k in range(TB):
                    ins = pe.transpose(ps[:, bank, k * P:(k + 1) * P],
                                       prob[:, i, k * P:(k + 1) * P], ident[:, :])
                ins.then_inc(pt_product, 1)

            def attend(n, sl, b, bank):
                d = slice(sl * P, (sl + 1) * P)
                for half in range(2):
                    pe.wait_ge(ptl_ready, 4 * n + 2 * half + 2)
                    cols = slice(half * 2 * P, (half + 1) * 2 * P)
                    for k in range(TB):
                        ins = three(ps[:, bank, cols], (vh[:, TB * b + k, d], vl[:, TB * b + k, d]),
                                    (pth[:, k, cols], ptl[:, k, cols]), k == 0, k == TB - 1)
                ins.then_inc(o_product, 1)

            def step(p, s, par, y_items=2, first=False):
                n = 4 * p + s
                sl, b = s % 2, s // 2
                pe.wait_ge(qk_lo_ready, n + 1)
                if not first:
                    pe.wait_ge(prob_ready, 4 * n)
                if y_items:
                    pe.wait_ge(y_added, 2 * n - 2)
                scores(n, sl)
                pair = p + 1 if b else p
                pe.wait_ge(wv_lo_ready, 2 * pair + 2)
                pe.wait_ge(vl_ready, n + 2)
                v_item(1 - par if b else par, TB * (1 - b) + 2 * sl, WORK)
                y_slot = par if b else 1 - par
                y_tile = (0 if b else TB) + 2 * sl
                for i in range(TB):
                    turn_probs(n, i)
                    if i == 1:
                        if first:
                            spread(1, (WORK + 1, SCORE))
                        else:
                            pe.wait_ge(otl_ready, n)
                        if y_items:
                            pe.wait_ge(wo_lo_ready, 2 * (p if b else p - 1) + 2)
                            y_item(y_slot, y_tile, SCORE)
                if y_items:
                    y_item(y_slot, y_tile + 1, SCORE + 1)
                if first:
                    pe.wait_ge(rms_row_ready, 4)
                else:
                    pe.wait_ge(vl_ready, n + 2 - sl)
                attend(n, sl, b, WORK + 1)

            step(0, 0, 0, y_items=0, first=True)
            step(0, 1, 0, y_items=0)

            def pair_steps(p, par):
                step(p, 2, par)
                step(p, 3, par)
                step(p + 1, 0, 1 - par)
                step(p + 1, 1, 1 - par)

            with pe.Fori(0, (PAIRS - 2) // 2) as i:
                pair_steps(2 * i, 0)
                pair_steps(2 * i + 1, 1)
            pair_steps(PAIRS - 2, 0)

            N = 4 * PAIRS - 2
            pe.wait_ge(qk_lo_ready, N + 1)
            pe.wait_ge(prob_ready, 4 * N)
            pe.wait_ge(y_added, 2 * N - 2)
            scores(N, 0)
            pe.wait_ge(vl_ready, N + 2)
            pe.wait_ge(otl_ready, N)
            pe.wait_ge(wo_lo_ready, 2 * PAIRS)
            for t, bank in enumerate((WORK, WORK + 1, TRANS, TRANS + 1)):
                y_item(1, t, bank)
            for i in range(2):
                pe.wait_ge(y_added, 2 * N + 1 + i)
                turn_probs(N, i)
            pe.wait_ge(qk_lo_ready, N + 2)
            pe.wait_ge(prob_ready, 4 * N + 4)
            scores(N + 1, 1)
            turn_probs(N, 2)
            turn_probs(N, 3)
            attend(N, 0, 1, WORK + 1)
            for i in range(TB):
                turn_probs(N + 1, i, LAST_TRANS[i])
            attend(N + 1, 1, 1, WORK)
            pe.wait_ge(otl_ready, N + 2)
            for i in range(TB):
                y_item(1, TB + i, SCORE + i)

            def turn_z(b, tiles):
                for k in tiles:
                    pe.wait_ge(z_ready[k % 2], 2 * b + k // 2 + 1)
                    for c in range(C):
                        ins = pe.transpose(ps[:, Z[b][k], c * P:(c + 1) * P],
                                           z[:, k, c * P:(c + 1) * P], ident[:, :])
                    ins.then_inc(z_turned, 1)

            def hidden(b):
                for k in range(TB):
                    t = TB * b + k
                    pe.wait_ge(zl_ready, t + 1)
                    cols = slice(t * P, (t + 1) * P)
                    half = slice(WIDE * (k % 2), WIDE * (k % 2 + 1))
                    for c in range(C):
                        rhs = slice(c * IN, c * IN + WIDE)
                        ins = three(ps[:, HIDDEN[b] + k // 2, half], (xh[:, c, cols], xl[:, c, cols]),
                                    (in_hi[:, rhs], in_lo[:, rhs]), c == 0, c == C - 1)
                ins.then_inc(hidden_ready, 1)

            def base(b, k, parts=range(C)):
                cols = slice((TB * b + k) * P, (TB * b + k + 1) * P)
                for c in parts:
                    three(ps[:, BASE[b][k], :], (xh[:, c, cols], xl[:, c, cols]),
                          (wb_hi[:, c, :], wb_lo[:, c, :]), c == 0, False)

            def turn_hw(b):
                pe.wait_ge(hw_ready, b + 1)
                for k in range(TB):
                    ins = pe.transpose(ps[:, HW[b], k * P:(k + 1) * P], hw[:, b, k * P:(k + 1) * P], ident[:, :])
                ins.then_inc(hw_turned, 1)

            def experts(b, k):
                pe.wait_ge(hw_lo_ready, b + 1)
                cols = slice(k * P, (k + 1) * P)
                three(ps[:, BASE[b][k], :], (hw_hi[:, b, cols], hw_lo[:, b, cols]), (bt_hi, bt_lo),
                      False, True).then_inc(ffn_product, 1)

            turn_z(0, range(TB))
            pe.wait_ge(ffn_lo_ready, 3)
            pe.wait_ge(y_added, 2 * N + 2 + TB)
            hidden(0)
            for k in range(TB):
                base(0, k)
            turn_hw(0)
            turn_z(1, (0, 1, 2))
            for k in range(TB):
                experts(0, k)
            turn_z(1, (3,))
            pe.wait_ge(ffn_read, 2)
            hidden(1)
            pe.wait_ge(ffn_read, TB)
            for k in range(3):
                base(1, k)
            turn_hw(1)
            base(1, 3, range(C // 2))
            for k in range(3):
                experts(1, k)
            base(1, 3, range(C // 2, C))
            experts(1, 3)

        @block.vector
        def _(dve):
            links, measured, roots = [0], [0], [0]

            def link(ins):
                links[0] += 1
                ins.then_inc(chain, 1)
                dve.wait_ge(chain, links[0])

            def tile_stats(src, stage, t):
                dve.bn_stats(stats[:, stage, t, :], src[:, t, :]).then_inc(stats_ready, 1)

            def tile_moments(stage, t):
                measured[0] += 1
                dve.wait_ge(stats_ready, measured[0])
                dve.bn_aggr(mv[:, stage, t, :], stats[:, stage, t, :]).then_inc(mv_ready, 1)

            def moments(src, stage, tiles, before=None):
                for j, t in enumerate(tiles):
                    if before:
                        before(t)
                    tile_stats(src, stage, t)
                    if j:
                        tile_moments(stage, tiles[j - 1])
                tile_moments(stage, tiles[-1])

            def variances(stage, t, k):
                tiles = slice(t, t + k)
                dve.wait_ge(mv_ready, measured[0])
                dve.tensor_scalar(var_eps[:, stage, tiles], mv[:, stage, tiles, 1], LN_EPS, None,
                                  ALU.add).then_inc(var_ready, 1)

            def wait_roots():
                roots[0] += 1
                dve.wait_ge(rstd_ready, roots[0])

            def offsets(stage, t, k):
                tiles = slice(t, t + k)
                wait_roots()
                dve.scalar_tensor_tensor(out=nmr[:, stage, tiles], in0=mv[:, stage, tiles, 0], scalar=-1.0,
                                         in1=rstd[:, stage, tiles], op0=ALU.mult,
                                         op1=ALU.mult).then_inc(nmr_ready, 1)

            def low_wa(par):
                dve.tensor_tensor(wa_lo[:, par], wa_stage[:, par], f32(wa_hi[:, par]),
                                  ALU.subtract).then_inc(wa_lo_ready, 1)

            def norm_x(b):
                for t in (TB * b, TB * b + 2):
                    moments(y, 0, (t, t + 1), before=lambda t: dve.wait_ge(x_loaded[t], 16))
                    variances(0, t, 2)
                for t in (TB * b + 1, TB * b + 3):
                    offsets(0, t - 1, 2)
                    dve.tensor_scalar(y[:, t, :], y[:, t, :], mv[:, 0, t, 0:1], rstd[:, 0, t:t + 1],
                                      ALU.subtract, ALU.mult).then_inc(x_normed[1], 1)

            def low_x(b):
                for t in range(TB * b, TB * b + TB):
                    dve.wait_ge(xh_ready, t + 1)
                    cols = slice(t * P, (t + 1) * P)
                    dve.tensor_tensor(xl[:, :, cols], ps[:, X[t], :].rearrange("p (c n) -> p c n", c=C),
                                      f32(xh[:, :, cols]), ALU.subtract).then_inc(xl_ready, 1)

            norm_x(0)
            dve.wait_ge(wa_hi_ready, 1)
            low_wa(0)
            low_x(0)
            dve.wait_ge(wa_hi_ready, 2)
            low_wa(1)
            norm_x(1)
            dve.wait_ge(tab_loaded, 16)

            def store_qk(par, g, h, count):
                w, b = g % 2, g // 2
                dve.wait_ge(sq_ready, count)
                dve.tensor_scalar(qk_out[:, par, w, b * S:(b + 1) * S], ps[:, 4 * par + g, :],
                                  tab[:, w, bass.ds(h, 1)], tab[:, 2 + w, bass.ds(h, 1)],
                                  ALU.add, ALU.mult).then_inc(qk_out_ready, 1)

            for pos, (par, g) in enumerate(BY_BATCH):
                store_qk(par, g, par, pos + 1)
                if pos == 2:
                    low_x(1)
                if pos == 5:
                    dve.wait_ge(wa_hi_ready, 3)
                    low_wa(0)

            def phase_a(i):
                for par in range(2):
                    h = 2 * i + par
                    dve.wait_ge(wa_hi_ready, h + 2)
                    low_wa(1 - par)
                    dve.wait_ge(stored[par], 16 * i)
                    for g in range(4):
                        store_qk(par, g, h, 4 * h + g + 1)

            with dve.Fori(1, PAIRS - 1) as i:
                phase_a(i)

            def mean_squares(b, bank):
                cols = slice(NT * b, NT * b + NT)
                dve.wait_ge(col_sums, b + 1)
                dve.tensor_scalar(sq_eps[:, cols], ps[:, bank, cols], 1.0 / INNER, RMS_EPS,
                                  ALU.mult, ALU.add).then_inc(var_ready, 1)

            def diagonals(b):
                dve.wait_ge(rms_ready, b + 1)
                for w in range(2):
                    for k in range(TB):
                        col = NT * b + TB * w + k
                        ins = dve.tensor_scalar(factors(b, w)[:, k * P:(k + 1) * P], ident[:, :],
                                                rms[:, col:col + 1], 1.0 if w else SCORE_SCALE,
                                                ALU.mult, ALU.mult)
                    ins.then_inc(diag_ready, 1)

            dve.wait_ge(wa_hi_ready, HEADS)
            low_wa(1)
            for pos, (par, g) in enumerate(BY_BATCH):
                if pos == 0 or pos == 2:
                    dve.wait_ge(stored[par], 16 * (PAIRS - 1))
                store_qk(par, g, HEADS - 2 + par, 8 * (PAIRS - 1) + pos + 1)
                if pos == 4:
                    mean_squares(0, 0)
                    diagonals(0)

            def split_v(item, tile, bank):
                dve.wait_ge(vh_ready, item)
                dve.tensor_tensor(vl[:, tile:tile + 2, :], ps[:, bank, :].rearrange("p (t n) -> p t n", t=2),
                                  f32(vh[:, tile:tile + 2, :]), ALU.subtract).then_inc(vl_ready, 1)

            split_v(1, 0, 1)
            mean_squares(1, 2)
            diagonals(1)
            split_v(2, 2, WORK + 1)
            dve.wait_ge(y_set, 16 * NT)
            dve.sem_inc(y_added, 2)

            def add_y(count, tile, bank):
                dve.wait_ge(y_product, count)
                return dve.tensor_tensor(y[:, tile, :], y[:, tile, :], ps[:, bank, :], ALU.add)

            def evacuate_o(h, s, n, bank=WORK + 1):
                sl, b = s % 2, s // 2
                cols = slice(b * S, (b + 1) * S)
                dve.wait_ge(oth_ready, n + 1)
                dve.scalar_tensor_tensor(out=otl[:, sl, cols], in0=ps[:, bank, :],
                                         scalar=tab[:, 4, bass.ds(h, 1)], in1=f32(oth[:, sl, cols]),
                                         op0=ALU.add, op1=ALU.subtract).then_inc(otl_ready, 1)

            def maximum(n, sl, i):
                dve.wait_ge(scores_ready, 4 * n + i + 1)
                dve.tensor_reduce(neg_max[:, sl, i:i + 1], ps[:, SCORE + i, :], AX.X, ALU.max,
                                  negate=True).then_inc(max_ready, 1)

            def normalize(n, sl, i):
                dve.wait_ge(exp_ready, 4 * n + i + 1)
                dve.reciprocal(row_inv[:, sl, i:i + 1], row_sum[:, sl, i:i + 1]).then_inc(inv_ready, 1)
                dve.wait_ge(inv_ready, 4 * n + i + 1)
                dve.tensor_scalar(prob[:, i, :], prob[:, i, :], row_inv[:, sl, i:i + 1], None,
                                  ALU.mult).then_inc(prob_ready, 1)

            def low_pt(n, i, bank=None):
                dve.wait_ge(pth_ready, 4 * n + i + 1)
                rows = slice(i * P, (i + 1) * P)
                dve.tensor_tensor(ptl[:, :, rows],
                                  ps[:, TRANS + i % 2 if bank is None else bank, :].rearrange(
                                      "p (k q) -> p k q", k=TB),
                                  f32(pth[:, :, rows]), ALU.subtract).then_inc(ptl_ready, 1)

            def step(p, s, y_items=2, first=False):
                n = 4 * p + s
                b, sl = s // 2, s % 2
                for i in range(TB):
                    maximum(n, sl, i)
                    if i == 1 and not first:
                        evacuate_o(2 * p + 1 - sl if s else 2 * p - 1, (s - 1) % 4, n - 1)
                for i in range(TB):
                    normalize(n, sl, i)
                for i in range(TB):
                    low_pt(n, i)
                    if i == 1:
                        split_v(n + 3, TB * (1 - b) + 2 * sl, WORK)
                for k in range(y_items):
                    add_y(2 * n - 3 + k, (0 if b else TB) + 2 * sl + k, SCORE + k).then_inc(y_added, 1)

            step(0, 0, y_items=0, first=True)
            step(0, 1, y_items=0)

            def pair_steps(p):
                step(p, 2)
                step(p, 3)
                step(p + 1, 0)
                step(p + 1, 1)

            with dve.Fori(0, (PAIRS - 2) // 2) as i:
                pair_steps(2 * i)
                pair_steps(2 * i + 1)
            pair_steps(PAIRS - 2)

            def add_x(t):
                if t % 2:
                    dve.wait_ge(x_added, t // 2 + 1)
                else:
                    if t % TB:
                        dve.wait_ge(y_normed, t - t // TB)
                    else:
                        link(dve.tensor_scalar(y[:, t, :], y[:, t, :], mv[:, 1, t, 0:1], rstd[:, 1, t:t + 1],
                                               ALU.subtract, ALU.mult))
                    dve.wait_ge(x_reloaded, 16 * NT)
                    link(dve.tensor_tensor(y[:, t, :], y[:, t, :], x_again[:, t, :], ALU.add))

            def make_z(b):
                for k in range(1, TB, 2):
                    t = TB * b + k
                    if b:
                        dve.wait_ge(z_turned, k + 1)
                    dve.tensor_scalar(z[:, k, :], y[:, t, :], mv[:, 2, t, 0:1], rstd[:, 2, t:t + 1],
                                      ALU.subtract, ALU.mult).then_inc(z_ready[1], 1)

            def low_z(k, b):
                t = TB * b + k
                dve.wait_ge(zh_ready, t + 1)
                cols = slice(t * P, (t + 1) * P)
                dve.tensor_tensor(xl[:, :, cols], ps[:, Z[b][k], :].rearrange("p (c n) -> p c n", c=C),
                                  f32(xh[:, :, cols]), ALU.subtract).then_inc(zl_ready, 1)

            def both(b):
                return ps[:, HIDDEN[b]:HIDDEN[b] + 2, :].rearrange("p j (i n) -> p (j i) n", n=WIDE)

            def over_experts(b, k):
                return g_s[:, k, TB * b:TB * b + TB].unsqueeze(2).broadcast_to([P, TB, E])

            def gate_arguments(b):
                gb = slice(TB * b, TB * b + TB)
                dve.wait_ge(hidden_ready, b + 1)
                link(dve.tensor_reduce(g_s[:, 2, gb], both(b)[:, :, P:P + E], AX.X, ALU.max))
                dve.tensor_tensor(g_e[:, gb, :], both(b)[:, :, P:P + E], over_experts(b, 2),
                                  ALU.subtract).then_inc(gate_in, 1)
                dve.tensor_scalar(g_s[:, 0, gb], both(b)[:, :, P + E], thr_bias[:, 0:1], None,
                                  ALU.add).then_inc(gate_in, 1)

            def gates(b):
                gb = slice(TB * b, TB * b + TB)
                dve.wait_ge(gate_exp, 2 * b + 2)
                dve.tensor_scalar(g_s[:, 5, gb], g_s[:, 1, gb], 8.0, 8.0, ALU.mult, ALU.add)
                link(dve.tensor_reduce(g_s[:, 3, gb], g_e[:, gb, :], AX.X, ALU.add))
                dve.reciprocal(g_s[:, 6, gb], g_s[:, 5, gb])
                link(dve.reciprocal(g_s[:, 4, gb], g_s[:, 3, gb]))
                link(dve.tensor_tensor(g_p[:, gb, :], g_e[:, gb, :], over_experts(b, 4), ALU.mult))
                link(dve.tensor_tensor(g_w[:, gb, :], g_p[:, gb, :], over_experts(b, 6), ALU.subtract))
                link(dve.tensor_scalar(g_p[:, gb, :], g_w[:, gb, :], 0.0, 2.0, ALU.max, ALU.mult))
                link(dve.tensor_reduce(g_s[:, 7, gb], g_p[:, gb, :], AX.X, ALU.add))
                link(dve.tensor_scalar(g_s[:, 8, gb], g_s[:, 7, gb], 0.0, None, ALU.is_equal))
                link(dve.scalar_tensor_tensor(out=g_s[:, 9, gb], in0=g_s[:, 7, gb], scalar=0.5,
                                              in1=g_s[:, 8, gb], op0=ALU.mult, op1=ALU.add))
                link(dve.reciprocal(g_s[:, 7, gb], g_s[:, 9, gb]))
                link(dve.tensor_tensor(g_w[:, gb, :], g_p[:, gb, :], over_experts(b, 7), ALU.mult))
                dve.tensor_tensor(hw[:, b, :].rearrange("p (t e r) -> p t e r", e=E, r=R),
                                  both(b)[:, :, 0:P].rearrange("p t (e r) -> p t e r", r=R),
                                  g_w[:, gb, :].unsqueeze(3).broadcast_to([P, TB, E, R]),
                                  ALU.mult).then_inc(hw_ready, 1)

            def low_hw(b):
                dve.wait_ge(hw_hi_ready, b + 1)
                dve.tensor_tensor(hw_lo[:, b, :], ps[:, HW[b], :], f32(hw_hi[:, b, :]),
                                  ALU.subtract).then_inc(hw_lo_ready, 1)

            def add_bias(t):
                dve.wait_ge(ffn_product, t + 1)
                return dve.tensor_tensor(x_again[:, t, :], ps[:, BASE[t // TB][t % TB], :], bb, ALU.add)

            def add_ffn(t):
                dve.wait_ge(ffn_normed, t + 1)
                dve.tensor_tensor(y[:, t, :], y[:, t, :], x_again[:, t, :], ALU.add).then_inc(out_ready[1], 1)

            N = 4 * PAIRS - 2
            added = 2 * N - 4
            maximum(N, 0, 0)
            maximum(N, 0, 1)
            evacuate_o(HEADS - 1, 1, N - 1)
            maximum(N, 0, 2)
            maximum(N, 0, 3)
            normalize(N, 0, 0)
            normalize(N, 0, 1)
            last_y = ((0, WORK), (1, WORK + 1), (2, TRANS), (3, TRANS + 1))
            for tile, bank in last_y[0:2]:
                add_y(added + tile + 1, tile, bank).then_inc(y_added, 1)
            normalize(N, 0, 2)
            normalize(N, 0, 3)
            for tile, bank in last_y[2:4]:
                add_y(added + tile + 1, tile, bank).then_inc(y_added, 1)
            dve.wait_ge(y_added, 2 * N + 2)
            tile_stats(y, 1, 0)
            low_pt(N, 0)
            low_pt(N, 1)
            for i in range(TB):
                maximum(N + 1, 1, i)
            low_pt(N, 2)
            low_pt(N, 3)
            for i in range(TB):
                normalize(N + 1, 1, i)
                if i == 1:
                    tile_stats(y, 1, 1)
            for i in range(TB):
                low_pt(N + 1, i, LAST_TRANS[i])
            tile_stats(y, 1, 2)
            tile_stats(y, 1, 3)
            for t in range(TB):
                tile_moments(1, t)
            variances(1, 0, TB)
            evacuate_o(HEADS - 2, 2, N)
            evacuate_o(HEADS - 1, 3, N + 1, bank=WORK)
            offsets(1, 0, TB)

            moments(y, 2, (0, 2, 1, 3), before=add_x)
            variances(2, 0, TB)
            for t in range(TB, TB + 2):
                add_y(added + t + 1, t, SCORE + t - TB).then_inc(y_added, 1)
            offsets(2, 0, TB)
            make_z(0)
            for t in range(TB + 2, NT):
                add_y(added + t + 1, t, SCORE + t - TB).then_inc(y_added, 1)
            dve.wait_ge(y_added, 2 * N + 2 + TB)
            moments(y, 1, range(TB, NT), before=lambda t: low_z(t - TB, 0))
            variances(1, TB, TB)
            offsets(1, TB, TB)
            gate_arguments(0)
            moments(y, 2, (TB, TB + 2, TB + 1, TB + 3), before=add_x)
            variances(2, TB, TB)
            gates(0)
            offsets(2, TB, TB)
            make_z(1)
            low_hw(0)
            for k in range(3):
                low_z(k, 1)
            dve.wait_ge(bb_loaded, 16)
            for t in range(TB):
                add_bias(t).then_inc(ffn_read, 1)
            low_z(3, 1)
            dve.wait_ge(ffn_read, TB)
            moments(x_again, 3, range(TB))
            variances(3, 0, TB)
            offsets(3, 0, TB)
            gate_arguments(1)
            gates(1)
            add_ffn(1)
            add_ffn(3)
            low_hw(1)
            for t in range(TB, NT):
                link(add_bias(t))
                moments(x_again, 3, (t,))
                variances(3, t, 1)
                if t > TB:
                    offsets(3, t - 1, 1)
            t = NT - 1
            link(dve.tensor_scalar(x_again[:, t, :], x_again[:, t, :], mv[:, 3, t, 0:1], None, ALU.subtract))
            add_ffn(TB + 1)
            wait_roots()
            dve.scalar_tensor_tensor(out=y[:, t, :], in0=x_again[:, t, :], scalar=rstd[:, 3, t:t + 1],
                                     in1=y[:, t, :], op0=ALU.mult, op1=ALU.add).then_inc(out_ready[1], 1)


def kernel(L0_attn_hidden_states, L0_attn_Wq, L0_attn_bq, L0_attn_Wk, L0_attn_bk, L0_attn_Wv, L0_attn_bv,
           L0_attn_Wo, L0_attn_bo, L0_attn_gq, L0_attn_gk, L0_ffn_W_base, L0_ffn_b_base, L0_ffn_W_gate,
           L0_ffn_W_thr, L0_ffn_b_thr, L0_ffn_A, L0_ffn_B):
    import numpy as np
    import concourse.bacc as bacc
    from concourse.bass_utils import run_bass_kernel_spmd

    x = np.asarray(L0_attn_hidden_states)
    D, C = x.shape[-1], x.shape[-1] // P
    inner = L0_attn_Wq.shape[1]
    heads = inner // P

    def by_head(w, n):
        return np.asarray(w).reshape(C, P, inner // n, n).transpose(2, 1, 0, 3)

    def chunks(w):
        return np.asarray(w).reshape(C, P, -1).transpose(1, 0, 2)

    def columns(v):
        return np.asarray(v).reshape(heads, P).T

    def on_all(v):
        return np.broadcast_to(np.asarray(v), (P, v.shape[0]))

    gate = np.concatenate([np.asarray(L0_ffn_W_gate), np.asarray(L0_ffn_W_thr)])
    a_gate = chunks(np.concatenate([np.asarray(L0_ffn_A).reshape(-1, D), gate]).T)
    pad = 2 * P - a_gate.shape[2]
    a_gate = np.concatenate([a_gate.reshape(P, -1), np.zeros((P, pad), a_gate.dtype)], axis=1)
    arrays = {
        "x": x.reshape(-1, P, D),
        "w_qk": np.stack([by_head(L0_attn_Wq, P), by_head(L0_attn_Wk, P)], axis=2),
        "w_v": by_head(L0_attn_Wv, 2 * P),
        "w_o": np.asarray(L0_attn_Wo).reshape(heads // 2, 2, P, D).transpose(0, 2, 1, 3),
        "tables": np.stack([columns(v) for v in (L0_attn_bq, L0_attn_bk, L0_attn_gq, L0_attn_gk, L0_attn_bv)],
                           axis=1),
        "bo": on_all(L0_attn_bo),
        "w_base": chunks(np.asarray(L0_ffn_W_base).T),
        "w_in": a_gate,
        "b_t": np.asarray(L0_ffn_B).transpose(0, 2, 1).reshape(P, -1),
        "b_base": on_all(L0_ffn_b_base),
        "b_thr": on_all(L0_ffn_b_thr),
    }
    nc = bacc.Bacc("TRN2", target_bir_lowering=False, num_devices=1)
    arrays = {name: np.ascontiguousarray(a) for name, a in arrays.items()}
    aps = [nc.dram_tensor(name, a.shape, mybir.dt.from_np(a.dtype), kind="ExternalInput").ap()
           for name, a in arrays.items()]
    out = nc.dram_tensor("out", arrays["x"].shape, F32, kind="ExternalOutput").ap()
    build(nc, *aps, out)
    r = run_bass_kernel_spmd(nc, [arrays], core_ids=[0])
    return r.results[0]["out"].reshape(x.shape)
```
